# Optimizing a Trainium2 kernel written in Bass

```python
import numpy as np
import jax
import jax.numpy as jnp

def _softmax(x, axis=-1):
    return jax.nn.softmax(x, axis=axis)

def _gelu(x):
    return jax.nn.gelu(x, approximate=True)

def _silu(x):
    return jax.nn.silu(x)

def _sigmoid(x):
    return jax.nn.sigmoid(x)

def _layernorm(x, axis=-1, eps=1e-05):
    m = jnp.mean(x, axis=axis, keepdims=True)
    v = jnp.var(x, axis=axis, keepdims=True)
    return (x - m) / jnp.sqrt(v + eps)

def _scatter_add(tgt, idx, src, axis=0):
    return tgt.at[idx].add(src)

def _segment_sum(src, seg, n):
    return jax.ops.segment_sum(src, seg, n)
kernel_name = 'mk_xattn_ffn_d1_seqx_r4_30f332'

def setup_inputs(seed: int=0):
    np.random.seed(seed)
    _w = jnp.asarray

    def _rec_inputs():
        import jax
        import jax.numpy as jnp
        _rk = jax.random.key(seed)
        x = -0.0002928 + 1 * jax.random.normal(jax.random.fold_in(_rk, 1), (8, 100, 256), jnp.float32)
        _lenS = 100 - jax.random.randint(jax.random.fold_in(_rk, 7), (8,), 0, max(1, 100 // 4) + 1, jnp.int32)
        _lenS2 = 361 - jax.random.randint(jax.random.fold_in(_rk, 8), (8,), 0, max(1, 361 // 4) + 1, jnp.int32)
        _ctx_1024P = jax.random.normal(jax.random.fold_in(_rk, 11), (8, 16, 256), jnp.float32)
        _ctx_1024c = jax.random.dirichlet(jax.random.fold_in(_rk, 511), 0.3 * jnp.ones((16,), jnp.float32), (8, 361))
        _ctx_1024t = jnp.einsum('bsk,bkd->bsd', _ctx_1024c, _ctx_1024P)
        _ctx_1024t = _ctx_1024t * jax.lax.rsqrt(jnp.mean(jnp.square(_ctx_1024t)) + 1e-12) * 0.953939
        ctx_1024 = -1.39393e-06 + 0.999914 * (_ctx_1024t + 0.3 * jax.random.normal(jax.random.fold_in(_rk, 611), (8, 361, 256), jnp.float32))
        return (x, ctx_1024)
    x, ctx_1024 = _rec_inputs()

    def _L0_xattn_setup():
        import jax, jax.numpy as jnp
        import numpy as np
        D_MODEL = 256
        NUM_HEADS = 16
        HEAD_DIM = D_MODEL // NUM_HEADS
        key = jax.random.key(seed)
        ks = jax.random.split(key, 10)
        B, SQ, SK = (2, 512, 512)
        scale = 1.0 / np.sqrt(D_MODEL)
        inp = {'x1': jax.random.normal(ks[0], (B, SQ, D_MODEL), jnp.float32), 'x2': jax.random.normal(ks[1], (B, SK, D_MODEL), jnp.float32), 'Wq': jax.random.normal(ks[2], (D_MODEL, D_MODEL), jnp.float32) * scale, 'bq': jnp.zeros((D_MODEL,), jnp.float32), 'Wk': jax.random.normal(ks[3], (D_MODEL, D_MODEL), jnp.float32) * scale, 'bk': jnp.zeros((D_MODEL,), jnp.float32), 'Wv': jax.random.normal(ks[4], (D_MODEL, D_MODEL), jnp.float32) * scale, 'bv': jnp.zeros((D_MODEL,), jnp.float32), 'Wo': jax.random.normal(ks[5], (D_MODEL, D_MODEL), jnp.float32) * scale, 'bo': jnp.zeros((D_MODEL,), jnp.float32)}
        return inp
    _L0_xattn_all = _L0_xattn_setup()
    _L0_xattn_in = {k: v for k, v in _L0_xattn_all.items() if k in ('Wq', 'bq', 'Wk', 'bk', 'Wv', 'bv', 'Wo', 'bo')}
    del _L0_xattn_all

    def _L0_ffn_setup():
        import jax, jax.numpy as jnp
        import numpy as np
        NUM_EXPERTS = 8
        TOP_K = 2

        def _swiglu(x, w1, w2, w3):
            return jax.nn.silu(x @ w1) * (x @ w3) @ w2
        key = jax.random.key(seed)
        ks = jax.random.split(key, 9)
        B, S, D, H, E = (1, 256, 256, 256, NUM_EXPERTS)
        std = 0.02
        return {'x': jax.random.normal(ks[0], (B, S, D), jnp.float32), 'router_w': jax.random.normal(ks[1], (D, E), jnp.float32) * std, 'expert_bias': jnp.zeros((E,), jnp.float32), 'w1': jax.random.normal(ks[2], (E, D, H), jnp.float32) * std, 'w2': jax.random.normal(ks[3], (E, H, D), jnp.float32) * std, 'w3': jax.random.normal(ks[4], (E, D, H), jnp.float32) * std, 'sw1': jax.random.normal(ks[5], (D, H), jnp.float32) * std, 'sw2': jax.random.normal(ks[6], (H, D), jnp.float32) * std, 'sw3': jax.random.normal(ks[7], (D, H), jnp.float32) * std}
    _L0_ffn_all = _L0_ffn_setup()
    _L0_ffn_in = {k: v for k, v in _L0_ffn_all.items() if k in ('router_w', 'expert_bias', 'w1', 'w2', 'w3', 'sw1', 'sw2', 'sw3')}
    del _L0_ffn_all
    return {'x': x, 'ctx_1024': ctx_1024, 'L0_xattn_Wq': _L0_xattn_in['Wq'], 'L0_xattn_bq': _L0_xattn_in['bq'], 'L0_xattn_Wk': _L0_xattn_in['Wk'], 'L0_xattn_bk': _L0_xattn_in['bk'], 'L0_xattn_Wv': _L0_xattn_in['Wv'], 'L0_xattn_bv': _L0_xattn_in['bv'], 'L0_xattn_Wo': _L0_xattn_in['Wo'], 'L0_xattn_bo': _L0_xattn_in['bo'], 'L0_ffn_router_w': _L0_ffn_in['router_w'], 'L0_ffn_expert_bias': _L0_ffn_in['expert_bias'], 'L0_ffn_w1': _L0_ffn_in['w1'], 'L0_ffn_w2': _L0_ffn_in['w2'], 'L0_ffn_w3': _L0_ffn_in['w3'], 'L0_ffn_sw1': _L0_ffn_in['sw1'], 'L0_ffn_sw2': _L0_ffn_in['sw2'], 'L0_ffn_sw3': _L0_ffn_in['sw3']}

def reference(x, ctx_1024, L0_xattn_Wq, L0_xattn_bq, L0_xattn_Wk, L0_xattn_bk, L0_xattn_Wv, L0_xattn_bv, L0_xattn_Wo, L0_xattn_bo, L0_ffn_router_w, L0_ffn_expert_bias, L0_ffn_w1, L0_ffn_w2, L0_ffn_w3, L0_ffn_sw1, L0_ffn_sw2, L0_ffn_sw3):
    import jax
    import jax.numpy as jnp

    def _L0_xattn_ref(x1, x2, Wq, bq, Wk, bk, Wv, bv, Wo, bo):
        import jax, jax.numpy as jnp
        import numpy as np
        D_MODEL = 256
        NUM_HEADS = 16
        HEAD_DIM = D_MODEL // NUM_HEADS
        B, SQ, _ = x1.shape
        SK = x2.shape[1]

        def split_heads(t, S):
            return t.reshape(B, S, NUM_HEADS, HEAD_DIM).transpose(0, 2, 1, 3)
        Q = split_heads(x1 @ Wq + bq, SQ)
        K = split_heads(x2 @ Wk + bk, SK)
        V = split_heads(x2 @ Wv + bv, SK)
        scores = jnp.einsum('bhqd,bhkd->bhqk', Q, K) / jnp.sqrt(jnp.asarray(HEAD_DIM, Q.dtype))
        attn = jax.nn.softmax(scores, axis=-1)
        ctx = jnp.einsum('bhqk,bhkd->bhqd', attn, V)
        ctx = ctx.transpose(0, 2, 1, 3).reshape(B, SQ, D_MODEL)
        return ctx @ Wo + bo

    def _L0_ffn_ref(x, router_w, expert_bias, w1, w2, w3, sw1, sw2, sw3):
        import jax, jax.numpy as jnp
        import numpy as np
        NUM_EXPERTS = 8
        TOP_K = 2

        def _swiglu(x, w1, w2, w3):
            return jax.nn.silu(x @ w1) * (x @ w3) @ w2
        B, S, D = x.shape
        E, K = (NUM_EXPERTS, TOP_K)
        N = B * S
        x_flat = x.reshape(N, D)
        logits = x_flat @ router_w
        scores = jax.nn.softmax(logits.astype(jnp.float32), axis=-1)
        _, sel = jax.lax.top_k(scores + expert_bias[None, :], K)
        top_scores = jnp.take_along_axis(scores, sel, axis=-1)
        flat_exp = sel.reshape(-1)
        order = jnp.argsort(flat_exp)
        exp_sorted = flat_exp[order]
        routed_input = x_flat[order // K]
        routed_output = jnp.zeros_like(routed_input)
        for e in range(E):
            mask = (exp_sorted == e)[:, None]
            y_e = _swiglu(routed_input, w1[e], w2[e], w3[e])
            routed_output = routed_output + jnp.where(mask, y_e, 0.0)
        unsorted = jnp.zeros((N * K, D), routed_output.dtype).at[order].set(routed_output)
        unsorted = unsorted.reshape(N, K, D)
        out_experts = jnp.einsum('nk,nkd->nd', top_scores, unsorted)
        shared_out = _swiglu(x_flat, sw1, sw2, sw3)
        return (shared_out + out_experts).reshape(B, S, D)
    x = x + _L0_xattn_ref(_layernorm(x, axis=-1), ctx_1024, L0_xattn_Wq, L0_xattn_bq, L0_xattn_Wk, L0_xattn_bk, L0_xattn_Wv, L0_xattn_bv, L0_xattn_Wo, L0_xattn_bo)
    x = x + _L0_ffn_ref(_layernorm(x, axis=-1), L0_ffn_router_w, L0_ffn_expert_bias, L0_ffn_w1, L0_ffn_w2, L0_ffn_w3, L0_ffn_sw1, L0_ffn_sw2, L0_ffn_sw3)
    return x

_drawn_inputs = setup_inputs


def setup_inputs(seed=0):
    import zlib

    import numpy as np

    out = dict(_drawn_inputs(seed))
    spreads = {'L0_xattn_bq': (0.0, 0.397),
     'L0_xattn_bk': (0.0, 0.8),
     'L0_xattn_bv': (0.0, 0.1),
     'L0_xattn_bo': (0.0, 0.1),
     'L0_ffn_expert_bias': (0.0, 0.8)}
    factors = {'L0_ffn_router_w': 8.0,
     'L0_ffn_w1': 8.0,
     'L0_ffn_w2': 8.0,
     'L0_ffn_w3': 8.0,
     'L0_ffn_sw1': 3.859,
     'L0_ffn_sw2': 3.803,
     'L0_ffn_sw3': 3.845}
    for name, (base, spread) in spreads.items():
        noise = np.random.default_rng([zlib.crc32(name.encode()), seed]).standard_normal(out[name].shape)
        drawn = base * np.exp(spread * noise) if base else spread * noise
        out[name] = jnp.asarray(drawn.astype(out[name].dtype))
    for name, factor in factors.items():
        out[name] = (out[name] * factor).astype(out[name].dtype)
    return out
```

```python
from contextlib import ExitStack
from typing import Any, NamedTuple

import concourse.bass as bass
from concourse import mybir

F32 = mybir.dt.float32
F32R = mybir.dt.float32r
BF16 = mybir.dt.bfloat16
I32 = mybir.dt.int32
U32 = mybir.dt.uint32
ACT = mybir.ActivationFunctionType
ALU = mybir.AluOpType
AX_X = mybir.AxisListType.X

P = 128
BANK = 512
EPS = 1e-5

PAIRS = [(0, 0), (0, 1), (1, 0), (1, 1), (0, 2), (2, 0)]
PARTS = 3
PASSES = [(0, 0), (1, 0), (0, 1)]


class Step(NamedTuple):
    pair: Any
    odd: int

    @property
    def n(self):
        return 2 * self.pair + self.odd

    def plus(self, k):
        return Step(self.pair + (self.odd + k) // 2, (self.odd + k) % 2)


def at(n):
    return Step(n // 2, n % 2)


def row(ap, n):
    return ap[bass.ds(n, 1)].rearrange("a r c -> (a r) c")


def wait_count(eng, sem, count):
    if isinstance(count, int) and count <= 0:
        return
    eng.wait_ge(sem, count)


def xattn_ffn(nc, x, ctx_in, wq, bq, wk, bk, wv, bv, wo, bo, router_w, expert_bias,
              w1, w2, w3, sw1, sw2, sw3, out):
    B, SQ, D = x.shape
    SK = ctx_in.shape[1]
    H = 16
    HD = D // H
    E, _, F = w1.shape
    KC = D // P
    FC = F // P
    TC = (SK + P - 1) // P
    SKP = TC * P
    LAST = SK - (TC - 1) * P
    SKE = SK + SK % 2
    HG = 4
    G = H // HG
    GQ = HG * SQ
    STACK = len(PAIRS) * HD
    ROWS = STACK + PARTS
    NT = B * SQ
    HALF = NT // 2
    HB = B // 2
    SCALE = HD ** -0.5
    NW = 3
    S_BANKS = TC

    with ExitStack() as ctx:
        def sb(name, shape, dt=F32):
            return ctx.enter_context(nc.sbuf_tensor(name, shape, dt))

        def sem(name):
            return ctx.enter_context(nc.semaphore(name))

        ident = sb("ident", [P, P])
        identb = sb("identb", [P, P], BF16)
        half_neg = sb("half_neg", [P, B])
        experts = sb("experts", [SQ, B, E])
        experts_i = sb("experts_i", [SQ, B, E], I32)
        wq_sb = sb("wq_sb", [P, KC, D])
        wkv_sb = sb("wkv_sb", [P, 2, KC, D])
        f32r_a = sb("f32r_a", [P, 2 * (2 * KC * D + KC * SKP)], F32R)

        def cut_a(offset, *dims):
            size = 1
            for n in dims:
                size *= n
            v = f32r_a[:, offset:offset + size]
            names = "abc"[:len(dims)]
            return v.rearrange(f"p ({' '.join(names)}) -> p {' '.join(names)}", **dict(zip(names, dims)))

        wkv_part = [cut_a(i * 2 * KC * D, 2, KC, D) for i in range(2)]
        wo_pad = sb("wo_pad", [P, G, D])
        bq_col = sb("bq_col", [P, KC])
        bk_col = sb("bk_col", [P, KC])
        bv_row = sb("bv_row", [P, 2, D])
        rw_sb = sb("rw_sb", [P, KC, E])
        rw_part = [sb(f"rw_part{i}", [P, KC, E], F32R) for i in range(2)]
        eb_row = sb("eb_row", [SQ, B, E])
        x_all = sb("x_all", [SQ, B, D])
        stats = sb("stats", [SQ, B, 6])
        mv = sb("mv", [SQ, B, 2])
        var_eps = sb("var_eps", [SQ, B])
        rstd = sb("rstd", [SQ, B])
        xn = sb("xn", [SQ, B, D])
        xnT = sb("xnT", [P, KC, NT])
        qf = sb("qf", [P, KC, NT])
        qr = sb("qr", [P, KC, NT])
        qp = sb("qp", [P, PARTS, KC, NT], BF16)
        qst_all = sb("qst_all", [STACK, H, NT], BF16)
        cx = [sb(f"cx{i}", [P, TC, D]) for i in range(2)]
        ct_part = [cut_a(4 * KC * D + i * KC * SKP, KC, SKP) for i in range(2)]
        kf = sb("kf", [P, KC, SK])
        kr = sb("kr", [P, KC, SK])
        kp = sb("kp", [P, PARTS, KC, SK], BF16)
        kst = [sb(f"kst{i}", [ROWS, H, SKP], BF16) for i in range(2)]
        qst = [sb(f"qst{i}", [ROWS, H, SQ], BF16) for i in range(2)]
        vaug = [sb(f"vaug{i}", [P, TC, H, 2 * HD]) for i in range(2)]
        negm = sb("negm", [SQ, H])
        negm_r = sb("negm_r", [SQ, H])
        mp = sb("mp", [SQ, PARTS, H], BF16)
        mts = sb("mts", [PARTS * H, SQ], BF16)
        probs = [sb(f"probs{i}", [P, TC, GQ]) for i in range(2)]
        den = sb("den", [P, G * SQ])
        ctxn = sb("ctxn", [P, G * SQ])
        xT_part = [sb(f"xT_part{i}", [P, KC, NT], F32R) for i in range(2)]
        logits = sb("logits", [SQ, B, E])
        rowmax = sb("rowmax", [SQ, B])
        ex = sb("ex", [SQ, B, E])
        esum = sb("esum", [SQ, B])
        erec = sb("erec", [SQ, B])
        score = sb("score", [SQ, B, E])
        biased = sb("biased", [SQ, B, E])
        top8 = sb("top8", [SQ, B, 8])
        top8_i = sb("top8_i", [SQ, B, 8], U32)
        top8_f = sb("top8_f", [SQ, B, 8])
        is_first = sb("is_first", [SQ, B, E])
        is_second = sb("is_second", [SQ, B, E])
        chosen = sb("chosen", [SQ, B, E])
        gate = sb("gate", [SQ, B, 1 + E])
        w_raw = [t[:, :, :].rearrange("p c t -> p (c t)")[:, 0:NW * KC * F].rearrange(
            "p (w c n) -> p w c n", w=NW, c=KC) for t in (xnT, qr)]
        w_part = [[sb(f"w_part{i}_{j}", [P, NW, KC, F], F32R) for j in range(2)] for i in range(2)]
        sil, hm = (qf[:, :, :].rearrange("p c t -> p (c t)")[:, i * FC * HALF:(i + 1) * FC * HALF].rearrange(
            "p (m t) -> p m t", m=FC) for i in range(2))
        h_part = [[cut_a((2 * i + j) * FC * HALF, FC, HALF) for j in range(2)] for i in range(2)]

        q_dram = nc.dram_tensor("q_parts", [PARTS, D, NT], BF16, kind="Internal").ap()
        k_dram = [nc.dram_tensor(f"k_parts{i}", [PARTS, D, SK], BF16, kind="Internal").ap() for i in range(2)]

        bank = [ctx.enter_context(nc.psum_tensor(f"bank{i}", [P, BANK], F32)) for i in range(8)]
        s_bank = bank[0:3]
        o_bank = bank[3]
        m_bank = bank[4:6]
        g_bank = bank[6:8]
        up_bank = [bank[0:2], bank[2:4]]
        y_bank = [bank[4:6], bank[6:8]]

        s_ones = sem("ident_base")
        s_ident = sem("ident_ready")
        s_const = sem("consts_ready")
        s_kones = sem("k_stack_ones")
        s_step = sem("shift_chain")
        s_nrm = sem("norm_chain")
        s_apart = sem("wait_apart")
        s_iota = sem("iota_ready")
        d_x = sem("x_in")
        d_wkv = sem("wkv_in")
        d_wq = sem("wq_in")
        d_bias = sem("bias_in")
        d_late = sem("late_consts_in")
        s_wkv_hi = sem("wkv_hi_ready")
        s_wkv_lo = sem("wkv_lo_ready")
        s_vec = sem("vector_chain")
        s_gp = sem("pool_chain")
        s_var = sem("var_ready")
        s_rstd = sem("rstd_ready")
        s_xn = sem("xn_ready")
        s_xt_mm = sem("xn_transposed")
        s_xt = sem("xnT_ready")
        s_q_mm = sem("q_projected")
        s_qf = sem("qf_ready")
        s_qp = sem("q_parts_ready")
        d_q = sem("q_parts_stored")
        d_qst = sem("q_stack_in")
        d_cx = [sem(f"ctx_in{i}") for i in range(2)]
        s_ct_mm = sem("ctx_transposed")
        s_ct_hi = sem("ctxT_hi_ready")
        s_ct_lo = sem("ctxT_lo_ready")
        s_k_mm = sem("k_projected")
        s_k_ev = sem("k_evacuated")
        s_v_mm = sem("v_projected")
        s_v_ev = sem("v_evacuated")
        s_kp = sem("k_parts_ready")
        d_k = sem("k_parts_stored")
        d_kst = [sem(f"k_stack_in{i}") for i in range(2)]
        s_qst = sem("q_stack_ready")
        s_m_mm = sem("max_scores_done")
        s_m_rd = sem("max_reduced")
        s_mp = sem("shift_parts_ready")
        s_mt_mm = sem("shift_transposed")
        s_mt_ev = sem("shift_evacuated")
        d_shift = [sem(f"shift_in{i}") for i in range(2)]
        s_s_mm = sem("scores_done")
        s_exp = sem("exp_done")
        s_pv = sem("pv_done")
        s_norm = sem("norm_done")
        s_o_mm = sem("attn_out_done")
        s_o_ev = sem("attn_out_added")
        s_xn2 = sem("xn2_ready")
        s_x2_mm = sem("xn2_transposed")
        s_x2_hi = sem("xn2T_hi_ready")
        s_x2_lo = sem("xn2T_lo_ready")
        s_rw_hi = sem("router_w_hi_ready")
        s_rw_lo = sem("router_w_lo_ready")
        s_lg_mm = sem("logits_done")
        s_lg = sem("logits_shifted")
        s_ex = sem("router_exp_done")
        d_w = [sem(f"w_in{i}") for i in range(2)]
        s_w_hi = sem("w_hi_ready")
        s_w_lo = sem("w_lo_ready")
        s_up = sem("up_done")
        s_sil = sem("silu_done")
        s_hm = sem("hidden_ready")
        s_h_hi = sem("h_hi_ready")
        s_h_lo = sem("h_lo_ready")
        s_dn = sem("down_done")
        s_acc = sem("y_added")
        d_out = sem("out_stored")

        EXP0 = S_BANKS
        PV0 = 2
        O0 = 1
        ACC0 = B

        block = ctx.enter_context(nc.Block())

        def half_batches(half):
            return range(half * HB, half * HB + HB)

        @block.sync
        def _(sp):
            def load_ctx(b):
                wait_count(sp, s_ct_mm, KC * (b.n - 1))
                sp.dma_start(cx[b.odd][:, 0:TC - 1, :], row(ctx_in, b.n)[0:(TC - 1) * P, :].rearrange(
                    "(c p) d -> p c d", p=P)).then_inc(d_cx[b.odd], 16)
                sp.dma_start(cx[b.odd][0:LAST, TC - 1, :], row(ctx_in, b.n)[(TC - 1) * P:SK, :]).then_inc(d_cx[b.odd], 16)

            def stack_k(b):
                sp.wait_ge(s_kp, b.n + 1)
                sp.dma_start(k_dram[b.odd].rearrange("q (c p) t -> p q c t", p=P), kp[:, :, :, :]).then_inc(d_k, 16)
                sp.wait_ge(s_kones, 4)
                sp.wait_ge(d_k, 16 * (b.n + 1))
                sp.sem_inc(s_apart, 1)
                wait_count(sp, s_s_mm, G * TC * (b.n - 1))
                for j, (part, _) in enumerate(PAIRS):
                    sp.dma_start(kst[b.odd][j * HD:(j + 1) * HD, :, 0:SK],
                                 k_dram[b.odd][part].rearrange("(h d) t -> d h t", d=HD)).then_inc(d_kst[b.odd], 16)

            def load_shift(b):
                sp.wait_ge(s_mt_ev, b.n + 1)
                for part in range(PARTS):
                    sp.dma_start(qst[b.odd][STACK + part:STACK + part + 1, :, :],
                                 mts[part * H:(part + 1) * H, :]).then_inc(d_shift[b.odd], 16)

            def load_expert(s, first, second, third):
                wait_count(sp, s_w_lo, s.n - 1)
                for i, w in enumerate((first, second, third)):
                    sp.dma_start(w_raw[s.odd][:, i, :, :], w.rearrange("(c p) n -> p c n", p=P)).then_inc(d_w[s.odd], 16)

            sp.dma_start(x_all[:, :, :], x.rearrange("b q d -> q b d")).then_inc(d_x, 16)
            sp.dma_start(wq_sb[:, :, :], wq.rearrange("(c p) n -> p c n", p=P)).then_inc(d_wq, 16)
            sp.dma_start(bq_col[:, :], bq.rearrange("(c p) -> p c", p=P), allow_slow_non_contiguous=True).then_inc(d_bias, 16)
            sp.dma_start(bk_col[:, :], bk.rearrange("(c p) -> p c", p=P), allow_slow_non_contiguous=True).then_inc(d_bias, 16)
            for i in range(2):
                sp.dma_start(bv_row[:, i, :], bv.partition_broadcast(P)).then_inc(d_bias, 16)
            sp.wait_ge(s_const, 2)
            load_ctx(at(0))
            sp.dma_start(wkv_sb[:, 0, :, :], wk.rearrange("(c p) n -> p c n", p=P)).then_inc(d_wkv, 16)
            sp.dma_start(wkv_sb[:, 1, :, :], wv.rearrange("(c p) n -> p c n", p=P)).then_inc(d_wkv, 16)
            load_ctx(at(1))
            sp.wait_ge(s_const, 3)
            for j in range(HG):
                sp.dma_start(wo_pad[32 * j:32 * j + HD, :, :],
                             wo.rearrange("(g j d) n -> j d g n", j=HG, d=HD)[j]).then_inc(d_late, 16)
            sp.dma_start(wo_pad[HD:HD + 1, 0, :], bo.rearrange("(a n) -> a n", a=1)).then_inc(d_late, 16)
            sp.dma_start(rw_sb[:, :, :], router_w.rearrange("(c p) e -> p c e", p=P)).then_inc(d_late, 16)
            for b in range(B):
                sp.dma_start(eb_row[:, b, :], expert_bias.partition_broadcast(SQ)).then_inc(d_late, 16)
            sp.wait_ge(s_qp, 1)
            for c in range(KC):
                sp.dma_start(q_dram[:, c * P:(c + 1) * P, :].rearrange("q p t -> p q t"), qp[:, :, c, :]).then_inc(d_q, 16)
            sp.wait_ge(d_q, 16 * KC)
            for j, (_, part) in enumerate(PAIRS):
                sp.dma_start(qst_all[j * HD:(j + 1) * HD, :, :],
                             q_dram[part].rearrange("(h d) t -> d h t", d=HD)).then_inc(d_qst, 16)
            stack_k(at(0))
            load_ctx(at(2))
            stack_k(at(1))
            load_shift(at(0))
            load_expert(at(0), sw1, sw3, sw2)
            load_expert(at(1), w1[0], w3[0], w2[0])

            def iteration(i, last_load=False):
                if not last_load:
                    load_ctx(i.plus(3))
                load_shift(i.plus(1))
                stack_k(i.plus(2))

            with sp.Fori(0, B // 2 - 2) as pair:
                iteration(Step(pair, 0))
                iteration(Step(pair, 1))
            iteration(at(B - 4))
            iteration(at(B - 3), last_load=True)
            load_shift(at(B - 1))

            with sp.Fori(0, E // 2 - 1) as pair:
                for odd in range(2):
                    s = Step(pair, odd).plus(2)
                    e = s.n - 1
                    load_expert(s, row(w1, e), row(w3, e), row(w2, e))
            load_expert(at(E), w1[E - 1], w3[E - 1], w2[E - 1])
            for half in range(2):
                for b in half_batches(half):
                    sp.wait_ge(s_acc, ACC0 + B * E + b + 1)
                    sp.dma_start(out[b], x_all[:, b, :]).then_inc(d_out, 16)
            sp.wait_ge(d_out, 16 * B)

        @block.gpsimd
        def _(gp):
            gp.memset(ident[:, :], 0.0).then_inc(s_ones, 1)
            gp.memset(identb[:, :], 0.0).then_inc(s_ones, 1)
            gp.wait_ge(s_ones, 2)
            for t in (ident, identb):
                gp.affine_select(out=t[:, :], in_=t[:, :], compare_op=ALU.not_equal, fill=1.0, base=0,
                                 pattern=[[-1, P]], channel_multiplier=1).then_inc(s_ident, 1)
            gp.memset(half_neg[:, :], -0.5).then_inc(s_gp, 1)
            gp.wait_ge(s_gp, 1)
            gp.wait_ge(s_var, 1)
            gp.tensor_tensor(rstd[:, :], var_eps[:, :], half_neg[0:SQ, :], ALU.pow).then_inc(s_rstd, 1)
            for i in range(2):
                gp.memset(vaug[i][:, :, :, :], 1.0).then_inc(s_gp, 1)
            gp.wait_ge(s_gp, 3)
            for i in range(2):
                v = vaug[i][:, TC - 1, :, :].rearrange("p h d -> p (h d)")
                gp.affine_select(out=v, in_=v, compare_op=ALU.is_ge, fill=0.0, base=LAST - 1,
                                 pattern=[[0, 2 * D]], channel_multiplier=-1).then_inc(s_gp, 1)
            gp.iota(experts_i[:, :, :], pattern=[[0, B], [1, E]], base=0, channel_multiplier=0).then_inc(s_iota, 1)

            for i in range(2):
                gp.memset(kst[i][:, :, SK:SKP], 0.0).then_inc(s_kones, 1)
            gp.wait_ge(s_kones, 2)
            for i in range(2):
                gp.memset(kst[i][STACK:ROWS, :, 0:SK], 1.0).then_inc(s_kones, 1)

            gp.wait_ge(s_kones, 4)

            def split_k(b):
                n = 2 * b.n + 5
                gp.wait_ge(s_k_ev, KC * (b.n + 1))
                gp.tensor_tensor(kr[:, :, :], kf[:, :, :], kp[:, 0, :, :], ALU.subtract).then_inc(s_gp, 1)
                gp.wait_ge(s_gp, n + 1)
                wait_count(gp, d_k, 16 * b.n)
                gp.sem_inc(s_apart, 1)
                gp.tensor_copy(kp[:, 1, :, :], kr[:, :, :]).then_inc(s_gp, 1)
                gp.wait_ge(s_gp, n + 2)
                gp.tensor_tensor(kp[:, 2, :, :], kr[:, :, :], kp[:, 1, :, :], ALU.subtract).then_inc(s_kp, 1)

            split_k(at(0))
            split_k(at(1))
            with gp.Fori(0, B // 2 - 1) as pair:
                split_k(Step(pair, 0).plus(2))
                split_k(Step(pair, 1).plus(2))

            gp.wait_ge(s_var, 2)
            gp.tensor_tensor(rstd[:, :], var_eps[:, :], half_neg[0:SQ, :], ALU.pow).then_inc(s_rstd, 1)

            def cut_weights(s):
                gp.wait_ge(s_w_hi, s.n + 1)
                wait_count(gp, s_dn, 2 * (s.n - 1))
                gp.tensor_tensor(w_part[s.odd][1][:, :, :, :], w_raw[s.odd][:, :, :, :],
                                 w_part[s.odd][0][:, :, :, :].bitcast(F32), ALU.subtract).then_inc(s_w_lo, 1)

            def cut_hidden(s, cut_next=True):
                for half in range(2):
                    if half == 1 and cut_next:
                        cut_weights(s.plus(1))
                    u = 2 * s.n + half
                    gp.wait_ge(s_h_hi, u + 1)
                    wait_count(gp, s_dn, u - 1)
                    gp.tensor_tensor(h_part[half][1][:, :, :], hm[:, :, :],
                                     h_part[half][0][:, :, :].bitcast(F32), ALU.subtract).then_inc(s_h_lo, 1)

            cut_weights(at(0))
            cut_hidden(at(0))
            with gp.Fori(0, E // 2 - 1) as pair:
                for odd in range(2):
                    cut_hidden(Step(pair, odd).plus(1))
            cut_hidden(at(E - 1))
            cut_hidden(at(E), cut_next=False)

        @block.scalar
        def _(act):
            act.sem_inc(s_exp, EXP0)
            act.wait_ge(d_wkv, 32)
            act.activation(wkv_part[0][:, :, :, :], wkv_sb[:, :, :, :], ACT.Copy).then_inc(s_wkv_hi, 1)
            for n in range(2 * KC):
                c, half = n // 2, n % 2
                act.wait_ge(s_xt_mm, n + 1)
                act.activation(xnT[:, c, half * HALF:(half + 1) * HALF], bank[n][:, 0:HALF], ACT.Copy).then_inc(s_xt, 1)
            act.wait_ge(d_bias, 64)
            for n in range(2 * KC):
                c, half = n // 2, n % 2
                act.wait_ge(s_q_mm, n + 1)
                act.activation(qf[:, c, half * HALF:(half + 1) * HALF], bank[4 + n][:, 0:HALF], ACT.Identity,
                               bias=bq_col[:, c:c + 1]).then_inc(s_qf, 1)

            def ctx_hi(b):
                wait_count(act, s_v_mm, 2 * b.n)
                for c in range(KC):
                    act.wait_ge(s_ct_mm, KC * b.n + c + 1)
                    act.activation(ct_part[0][:, c, :], g_bank[c][:, 0:SKP], ACT.Copy).then_inc(s_ct_hi, 1)

            def evacuate_k(b):
                wait_count(act, s_kp, b.n)
                wait_count(act, d_k, 16 * b.n)
                for c in range(KC):
                    act.wait_ge(s_k_mm, KC * b.n + c + 1)
                    act.activation(kf[:, c, :], g_bank[1 - c][:, 0:SK], ACT.Identity, bias=bk_col[:, c:c + 1])
                    act.activation(kp[:, 0, c, :], g_bank[1 - c][:, 0:SK], ACT.Identity,
                                   bias=bk_col[:, c:c + 1]).then_inc(s_k_ev, 1)

            def evacuate_shift(b):
                act.wait_ge(s_mt_mm, b.n + 1)
                if not (isinstance(b.pair, int) and b.n == 0):
                    before = b.plus(-1)
                    act.wait_ge(d_shift[before.odd], 16 * PARTS * (before.pair + 1))
                act.activation(mts[:, :], g_bank[0][0:PARTS * H, 0:SQ // 2].bitcast(BF16), ACT.Copy).then_inc(s_mt_ev, 1)

            def exponentials(b):
                for g in range(G):
                    act.wait_ge(s_pv, G * b.n + g - 1 + PV0)
                    for c in range(TC):
                        act.wait_ge(s_s_mm, TC * (G * b.n + g) + c + 1)
                        act.activation(probs[g % 2][:, c, :], s_bank[c][:, 0:GQ], ACT.Exp, scale=SCALE).then_inc(s_exp, 1)

            ctx_hi(at(0))
            evacuate_k(at(0))
            ctx_hi(at(1))
            evacuate_k(at(1))
            evacuate_shift(at(0))

            def iteration(i):
                exponentials(i)
                ctx_hi(i.plus(2))
                evacuate_shift(i.plus(1))
                evacuate_k(i.plus(2))

            with act.Fori(0, B // 2 - 1) as pair:
                iteration(Step(pair, 0))
                iteration(Step(pair, 1))
            exponentials(at(B - 2))
            evacuate_shift(at(B - 1))
            exponentials(at(B - 1))

            act.wait_ge(d_late, 16 * (HG + 2 + B))
            act.activation(rw_part[0][:, :, :], rw_sb[:, :, :], ACT.Copy).then_inc(s_rw_hi, 1)

            def weights_hi(s):
                act.wait_ge(d_w[s.odd], 16 * NW * (s.pair + 1))
                wait_count(act, s_dn, 2 * (s.n - 1))
                act.activation(w_part[s.odd][0][:, :, :, :], w_raw[s.odd][:, :, :, :], ACT.Copy).then_inc(s_w_hi, 1)

            weights_hi(at(0))
            for n in range(2 * KC):
                c, half = n // 2, n % 2
                act.wait_ge(s_x2_mm, n + 1)
                act.activation(xT_part[0][:, c, half * HALF:(half + 1) * HALF], bank[n][:, 0:HALF],
                               ACT.Copy).then_inc(s_x2_hi, 1)
            act.wait_ge(s_lg, 1)
            act.activation(ex[:, :, :], logits[:, :, :], ACT.Exp).then_inc(s_ex, 1)

            def expert(s, cut_next=True):
                for half in range(2):
                    if half == 1 and cut_next:
                        weights_hi(s.plus(1))
                    u = 2 * s.n + half
                    wait_count(act, s_hm, FC * u)
                    for m in range(FC):
                        act.wait_ge(s_up, FC * u + m + 1)
                        act.activation(sil[:, m, :], up_bank[m][0][:, 0:HALF], ACT.Silu).then_inc(s_sil, 1)
                    act.wait_ge(s_hm, FC * (u + 1))
                    wait_count(act, s_dn, u - 1)
                    act.activation(h_part[half][0][:, :, :], hm[:, :, :], ACT.Copy).then_inc(s_h_hi, 1)

            expert(at(0))
            with act.Fori(0, E // 2 - 1) as pair:
                for odd in range(2):
                    expert(Step(pair, odd).plus(1))
            expert(at(E - 1))
            expert(at(E), cut_next=False)

        @block.tensor
        def _(pe):
            def ctx_transposes(b):
                pe.wait_ge(d_cx[b.odd], 32 * (b.pair + 1))
                for c in range(KC):
                    wait_count(pe, s_v_ev, 2 * b.n)
                    wait_count(pe, s_o_ev, b.n - 2 + O0)
                    wait_count(pe, s_mt_ev, b.n - 1)
                    for t in range(TC):
                        mm = pe.transpose(g_bank[c][:, t * P:(t + 1) * P], cx[b.odd][:, t, c * P:(c + 1) * P], ident[:, :])
                    mm.then_inc(s_ct_mm, 1)

            def project_k(b):
                pe.wait_ge(s_ct_lo, KC * (b.n + 1))
                for m in range(KC):
                    n = 0
                    for c in range(KC):
                        for wi, ci in PASSES:
                            mm = pe.matmul(g_bank[1 - m][:, 0:SKE], wkv_part[wi][:, 0, c, m * P:(m + 1) * P],
                                           ct_part[ci][:, c, 0:SKE], start=(n == 0), stop=(n == KC * len(PASSES) - 1))
                            n += 1
                    mm.then_inc(s_k_mm, 1)

            def project_v(b):
                for t in range(TC):
                    if t == 0:
                        pe.wait_ge(s_k_ev, KC * b.n + 1)
                    if t == TC - 1:
                        pe.wait_ge(s_k_ev, KC * b.n + 2)
                    dst = g_bank[1][:, t * D:(t + 1) * D] if t < TC - 1 else g_bank[0][:, 0:D]
                    n = 0
                    for c in range(KC):
                        for ci, wi in PASSES:
                            mm = pe.matmul(dst, ct_part[ci][:, c, t * P:(t + 1) * P], wkv_part[wi][:, 1, c, :],
                                           start=(n == 0), stop=(n == KC * len(PASSES) - 1))
                            n += 1
                    if t >= TC - 2:
                        mm.then_inc(s_v_mm, 1)

            def max_scores(b, h):
                wait_count(pe, s_m_rd, H * b.n + h - 1)
                pe.matmul(m_bank[h % 2][0:SQ, 0:SK], qst[b.odd][0:STACK, h, :], kst[b.odd][0:STACK, h, 0:SK],
                          start=True, stop=True).then_inc(s_m_mm, 1)

            def max_ready(b):
                pe.wait_ge(d_kst[b.odd], 16 * len(PAIRS) * (b.pair + 1))
                pe.wait_ge(s_qst, b.n + 1)

            def shift_transpose(b):
                pe.wait_ge(s_mp, b.n + 1)
                pe.sem_inc(s_apart, 1)
                pe.transpose(g_bank[0][0:PARTS * H, 0:SQ // 2].bitcast(BF16),
                             mp[:, :, :].rearrange("q s h -> q (s h)"), identb[0:SQ, 0:SQ]).then_inc(s_mt_mm, 1)

            def scores(b, g):
                for c in range(TC):
                    pe.wait_ge(s_exp, TC * (G * b.n + g) + c + 1 - TC + EXP0)
                    for j in range(HG):
                        h = HG * g + j
                        mm = pe.matmul(s_bank[c][:, j * SQ:(j + 1) * SQ], kst[b.odd][0:ROWS, h, c * P:(c + 1) * P],
                                       qst[b.odd][0:ROWS, h, :], start=True, stop=True)
                    mm.then_inc(s_s_mm, 1)

            def context(b, g):
                for c in range(TC):
                    pe.wait_ge(s_exp, TC * (G * b.n + g) + c + 1 + EXP0)
                    for j in range(HG):
                        mm = pe.matmul(o_bank[32 * j:32 * j + 32, g * SQ:(g + 1) * SQ],
                                       vaug[b.odd][:, c, HG * g + j, :], probs[g % 2][:, c, j * SQ:(j + 1) * SQ],
                                       start=(c == 0), stop=(c == TC - 1))
                mm.then_inc(s_pv, 1)

            def attn_out(b, bank_free):
                pe.wait_ge(s_norm, b.n + 1 + O0)
                sem_, count = bank_free
                pe.wait_ge(sem_, count)
                for g in range(G):
                    mm = pe.matmul(g_bank[1][0:SQ, 0:D], ctxn[:, g * SQ:(g + 1) * SQ], wo_pad[:, g, :],
                                   start=(g == 0), stop=(g == G - 1))
                mm.then_inc(s_o_mm, 1)

            pe.sem_inc(s_pv, PV0)
            pe.sem_inc(s_o_mm, O0)
            pe.wait_ge(s_ident, 2)
            for n in range(2 * KC):
                c, half = n // 2, n % 2
                pe.wait_ge(s_xn, B)
                for j, b in enumerate(half_batches(half)):
                    mm = pe.transpose(bank[n][:, j * SQ:(j + 1) * SQ], xn[:, b, c * P:(c + 1) * P], ident[0:SQ, 0:SQ])
                mm.then_inc(s_xt_mm, 1)
            pe.wait_ge(d_wq, 16)
            pe.wait_ge(s_xt, 2 * KC)
            for n in range(2 * KC):
                m, half = n // 2, n % 2
                for c in range(KC):
                    mm = pe.matmul(bank[4 + n][:, 0:HALF], wq_sb[:, c, m * P:(m + 1) * P],
                                   xnT[:, c, half * HALF:(half + 1) * HALF], start=(c == 0), stop=(c == KC - 1))
                mm.then_inc(s_q_mm, 1)
            pe.wait_ge(s_qf, 2 * KC)
            ctx_transposes(at(0))
            pe.wait_ge(s_wkv_lo, 1)
            project_k(at(0))
            project_v(at(0))
            ctx_transposes(at(1))
            project_k(at(1))
            project_v(at(1))
            max_ready(at(0))
            for h in range(H):
                max_scores(at(0), h)
            pe.wait_ge(s_v_ev, 4)
            shift_transpose(at(0))

            def iteration(i):
                pe.wait_ge(d_shift[i.odd], 16 * PARTS * (i.pair + 1))
                for g in range(G):
                    scores(i, g)
                    if g == 0:
                        max_ready(i.plus(1))
                    for h in range(HG * g, HG * (g + 1)):
                        max_scores(i.plus(1), h)
                    if g == 0:
                        pe.wait_ge(s_v_ev, 2 * (i.n + 1))
                        pe.wait_ge(s_norm, i.n + O0)
                    else:
                        context(i, g - 1)
                ctx_transposes(i.plus(2))
                context(i, G - 1)
                pe.wait_ge(s_ct_lo, KC * (i.n + 2) + 1)
                shift_transpose(i.plus(1))
                pe.wait_ge(s_mt_ev, i.n + 2)
                project_k(i.plus(2))
                project_v(i.plus(2))
                attn_out(i, (s_v_ev, 2 * (i.n + 2) + 1))

            pe.wait_ge(d_late, 16 * (HG + 2 + B))
            with pe.Fori(0, B // 2 - 1) as pair:
                iteration(Step(pair, 0))
                iteration(Step(pair, 1))
            i = at(B - 2)
            pe.wait_ge(d_shift[i.odd], 16 * PARTS * (i.pair + 1))
            pe.wait_ge(s_norm, i.n + O0)
            for g in range(G):
                scores(i, g)
                if g == 0:
                    max_ready(i.plus(1))
                for h in range(HG * g, HG * (g + 1)):
                    max_scores(i.plus(1), h)
                if g:
                    context(i, g - 1)
            context(i, G - 1)
            pe.wait_ge(s_v_ev, 2 * B)
            shift_transpose(i.plus(1))
            attn_out(i, (s_o_ev, B - 2 + O0))
            i = at(B - 1)
            pe.wait_ge(d_shift[i.odd], 16 * PARTS * (i.pair + 1))
            pe.wait_ge(s_norm, i.n + O0)
            for g in range(G):
                scores(i, g)
                if g:
                    context(i, g - 1)
            context(i, G - 1)
            attn_out(i, (s_o_ev, B - 1 + O0))

            pe.wait_ge(s_exp, TC * G * B + EXP0)
            pe.wait_ge(s_norm, B + O0)
            for n in range(2 * KC):
                c, half = n // 2, n % 2
                pe.wait_ge(s_xn2, B)
                for j, b in enumerate(half_batches(half)):
                    mm = pe.transpose(bank[n][:, j * SQ:(j + 1) * SQ], xn[:, b, c * P:(c + 1) * P], ident[0:SQ, 0:SQ])
                mm.then_inc(s_x2_mm, 1)
            pe.wait_ge(s_x2_lo, 2 * KC)
            pe.wait_ge(s_m_rd, H * B)
            pe.wait_ge(s_rw_lo, 1)
            for b in range(B):
                n = 0
                for c in range(KC):
                    for xi, wi in PASSES:
                        mm = pe.matmul(m_bank[0][0:SQ, b * E:(b + 1) * E], xT_part[xi][:, c, b * SQ:(b + 1) * SQ],
                                       rw_part[wi][:, c, :], start=(n == 0), stop=(n == KC * len(PASSES) - 1))
                        n += 1
            mm.then_inc(s_lg_mm, 1)

            def up(s, half):
                u = 2 * s.n + half
                if half == 0:
                    pe.wait_ge(s_w_lo, s.n + 1)
                for m in range(FC):
                    wait_count(pe, s_hm, FC * (u - 1) + m + 1)
                    for w in range(2):
                        n = 0
                        for c in range(KC):
                            for wi, xi in PASSES:
                                mm = pe.matmul(up_bank[m][w][:, 0:HALF], w_part[s.odd][wi][:, w, c, m * P:(m + 1) * P],
                                               xT_part[xi][:, c, half * HALF:(half + 1) * HALF],
                                               start=(n == 0), stop=(n == KC * len(PASSES) - 1))
                                n += 1
                    mm.then_inc(s_up, 1)

            def down(s, half):
                u = 2 * s.n + half
                pe.wait_ge(s_h_lo, u + 1)
                pe.wait_ge(s_acc, ACC0 + B * (s.n - 1) + HB * (half + 1))
                for j in range(HB):
                    n = 0
                    for c in range(FC):
                        for hi, wi in PASSES:
                            mm = pe.matmul(y_bank[half][j // 2][0:SQ, (j % 2) * D:(j % 2 + 1) * D],
                                           h_part[half][hi][:, c, j * SQ:(j + 1) * SQ], w_part[s.odd][wi][:, 2, c, :],
                                           start=(n == 0), stop=(n == FC * len(PASSES) - 1))
                            n += 1
                mm.then_inc(s_dn, 1)

            up(at(0), 0)
            up(at(0), 1)
            pe.wait_ge(s_lg, 1)
            pe.wait_ge(s_o_ev, B + O0)
            down(at(0), 0)
            with pe.Fori(0, E // 2) as pair:
                for odd in range(2):
                    s = Step(pair, odd).plus(1)
                    up(s, 0)
                    down(s.plus(-1), 1)
                    up(s, 1)
                    down(s, 0)
            down(at(E), 1)

        @block.vector
        def _(ve):
            chain = [0]

            def link(ins):
                chain[0] += 1
                ins.then_inc(s_vec, 1)
                ve.wait_ge(s_vec, chain[0])

            ve.sem_inc(s_norm, O0)
            ve.sem_inc(s_o_ev, O0)
            for i in range(2):
                ve.memset(cx[i][:, TC - 1, :], 0.0).then_inc(s_const, 1)
            ve.memset(wo_pad[:, :, :], 0.0).then_inc(s_const, 1)

            def layer_norm(dst, ready, round_):
                for b in range(B - 1):
                    ve.bn_stats(stats[:, b, :], x_all[:, b, :])
                link(ve.bn_stats(stats[:, B - 1, :], x_all[:, B - 1, :]))
                for b in range(B - 1):
                    ve.bn_aggr(mv[:, b, :], stats[:, b, :])
                link(ve.bn_aggr(mv[:, B - 1, :], stats[:, B - 1, :]))
                ve.tensor_scalar(var_eps[:, :], mv[:, :, 1], EPS, None, ALU.add).then_inc(s_var, 1)
                ve.wait_ge(s_rstd, round_)
                for b in range(B):
                    ve.tensor_scalar(dst[:, b, :], x_all[:, b, :], mv[:, b, 0:1], rstd[:, b:b + 1],
                                     ALU.subtract, ALU.mult).then_inc(ready, 1)

            ve.wait_ge(d_x, 16)
            layer_norm(xn, s_xn, 1)
            ve.wait_ge(s_wkv_hi, 1)
            ve.tensor_tensor(wkv_part[1][:, :, :, :], wkv_sb[:, :, :, :], wkv_part[0][:, :, :, :].bitcast(F32),
                             ALU.subtract).then_inc(s_wkv_lo, 1)
            ve.wait_ge(s_qf, 2 * KC)
            link(ve.tensor_copy(qp[:, 0, :, :], qf[:, :, :]))
            link(ve.tensor_tensor(qr[:, :, :], qf[:, :, :], qp[:, 0, :, :], ALU.subtract))
            link(ve.tensor_copy(qp[:, 1, :, :], qr[:, :, :]))
            ve.tensor_tensor(qp[:, 2, :, :], qr[:, :, :], qp[:, 1, :, :], ALU.subtract).then_inc(s_qp, 1)

            def ctx_lo(b):
                for c in range(KC):
                    ve.wait_ge(s_ct_hi, KC * b.n + c + 1)
                    ve.tensor_tensor(ct_part[1][:, c, :], g_bank[c][:, 0:SKP],
                                     ct_part[0][:, c, :].bitcast(F32), ALU.subtract).then_inc(s_ct_lo, 1)

            def evacuate_v(b):
                wait_count(ve, s_pv, G * (b.n - 1) + PV0)
                ve.wait_ge(s_v_mm, 2 * b.n + 1)
                ve.tensor_tensor(vaug[b.odd][:, 0:TC - 1, :, 0:HD],
                                 g_bank[1][:, 0:(TC - 1) * D].rearrange("p (c h d) -> p c h d", h=H, d=HD),
                                 bv_row[:, :, :].rearrange("p c (h d) -> p c h d", d=HD), ALU.add).then_inc(s_v_ev, 1)
                ve.wait_ge(s_v_mm, 2 * b.n + 2)
                ve.tensor_tensor(vaug[b.odd][0:LAST, TC - 1, :, 0:HD],
                                 g_bank[0][0:LAST, 0:D].rearrange("p (h d) -> p h d", d=HD),
                                 bv_row[0:LAST, 0, :].rearrange("p (h d) -> p h d", d=HD), ALU.add).then_inc(s_v_ev, 1)

            def stack_q(b):
                wait_count(ve, s_s_mm, G * TC * (b.n - 1))
                ve.tensor_copy(qst[b.odd][0:STACK, :, :],
                               qst_all[:, :, bass.ds(b.n * SQ, SQ)]).then_inc(s_qst, 1)

            def reduce_max(b, h):
                ve.wait_ge(s_m_mm, H * b.n + h + 1)
                ve.tensor_reduce(negm[:, h:h + 1], m_bank[h % 2][0:SQ, 0:SK], AX_X, ALU.max,
                                 negate=True).then_inc(s_m_rd, 1)

            def cut_shift(b):
                n = 3 * b.n
                ve.wait_ge(s_m_rd, H * (b.n + 1))
                wait_count(ve, s_mt_mm, b.n)
                ve.tensor_copy(mp[:, 0, :], negm[:, :]).then_inc(s_step, 1)
                ve.wait_ge(s_step, n + 1)
                ve.tensor_tensor(negm_r[:, :], negm[:, :], mp[:, 0, :], ALU.subtract).then_inc(s_step, 1)
                ve.wait_ge(s_step, n + 2)
                ve.tensor_copy(mp[:, 1, :], negm_r[:, :]).then_inc(s_step, 1)
                ve.wait_ge(s_step, n + 3)
                ve.tensor_tensor(mp[:, 2, :], negm_r[:, :], mp[:, 1, :], ALU.subtract).then_inc(s_mp, 1)

            def normalise(b):
                n = 2 * b.n
                ve.wait_ge(s_pv, G * (b.n + 1) + PV0)
                ve.sem_inc(s_apart, 1)
                ve.stream_shuffle(den[:, :], o_bank[:, 0:G * SQ],
                                  [HD + i % HD for i in range(32)]).then_inc(s_nrm, 1)
                ve.wait_ge(s_nrm, n + 1)
                ve.reciprocal(den[:, :], den[:, :]).then_inc(s_nrm, 1)
                ve.wait_ge(s_nrm, n + 2)
                ve.wait_ge(s_o_mm, b.n + O0)
                ve.tensor_tensor(ctxn[:, :], o_bank[:, 0:G * SQ], den[:, :], ALU.mult).then_inc(s_norm, 1)

            def add_attn_out(b):
                ve.wait_ge(s_o_mm, b.n + 1 + O0)
                row = x_all[:, bass.ds(b.n, 1), :].rearrange("q a d -> q (a d)")
                ve.tensor_tensor(row, g_bank[1][0:SQ, 0:D], row, ALU.add).then_inc(s_o_ev, 1)

            ve.wait_ge(s_gp, 5)
            ve.wait_ge(d_bias, 64)
            ctx_lo(at(0))
            evacuate_v(at(0))
            ctx_lo(at(1))
            evacuate_v(at(1))
            ve.wait_ge(d_qst, 16 * len(PAIRS))
            stack_q(at(0))
            stack_q(at(1))
            for h in range(H):
                reduce_max(at(0), h)
            cut_shift(at(0))

            def iteration(i):
                for h in range(H):
                    reduce_max(i.plus(1), h)
                cut_shift(i.plus(1))
                ctx_lo(i.plus(2))
                normalise(i)
                evacuate_v(i.plus(2))
                add_attn_out(i)
                stack_q(i.plus(2))

            with ve.Fori(0, B // 2 - 1) as pair:
                iteration(Step(pair, 0))
                iteration(Step(pair, 1))
            for h in range(H):
                reduce_max(at(B - 1), h)
            cut_shift(at(B - 1))
            normalise(at(B - 2))
            add_attn_out(at(B - 2))
            ve.wait_ge(d_late, 16 * (HG + 2 + B))
            normalise(at(B - 1))
            ve.wait_ge(s_rw_hi, 1)
            ve.tensor_tensor(rw_part[1][:, :, :], rw_sb[:, :, :], rw_part[0][:, :, :].bitcast(F32),
                             ALU.subtract).then_inc(s_rw_lo, 1)
            ve.wait_ge(s_iota, 1)
            link(ve.tensor_copy(experts[:, :, :], experts_i[:, :, :]))
            add_attn_out(at(B - 1))
            ve.wait_ge(s_o_ev, B + O0)
            ve.sem_inc(s_acc, ACC0)
            layer_norm(xn, s_xn2, 2)
            for n in range(2 * KC):
                c, half = n // 2, n % 2
                cols = slice(half * HALF, (half + 1) * HALF)
                ve.wait_ge(s_x2_hi, n + 1)
                ve.tensor_tensor(xT_part[1][:, c, cols], bank[n][:, 0:HALF], xT_part[0][:, c, cols].bitcast(F32),
                                 ALU.subtract).then_inc(s_x2_lo, 1)

            def wide(t):
                return t.unsqueeze(2).to_broadcast([SQ, B, E])

            ve.wait_ge(s_lg_mm, 1)
            lg = m_bank[0][0:SQ, 0:B * E].rearrange("q (b e) -> q b e", e=E)
            link(ve.tensor_reduce(rowmax[:, :], lg, AX_X, ALU.max))
            ve.tensor_tensor(logits[:, :, :], lg, wide(rowmax[:, :]), ALU.subtract).then_inc(s_lg, 1)
            ve.wait_ge(s_ex, 1)
            link(ve.tensor_reduce(esum[:, :], ex[:, :, :], AX_X, ALU.add))
            link(ve.reciprocal(erec[:, :], esum[:, :]))
            link(ve.tensor_tensor(score[:, :, :], ex[:, :, :], wide(erec[:, :]), ALU.mult))
            link(ve.tensor_tensor(biased[:, :, :], score[:, :, :], eb_row[:, :, :], ALU.add))
            for b in range(B - 1):
                ve.max(top8[:, b, :], biased[:, b, :])
            link(ve.max(top8[:, B - 1, :], biased[:, B - 1, :]))
            for b in range(B - 1):
                ve.max_index(top8_i[:, b, :], top8[:, b, :], biased[:, b, :])
            link(ve.max_index(top8_i[:, B - 1, :], top8[:, B - 1, :], biased[:, B - 1, :]))
            link(ve.tensor_copy(top8_f[:, :, :], top8_i[:, :, :]))
            link(ve.tensor_tensor(is_first[:, :, :], experts[:, :, :],
                                  top8_f[:, :, 0:1].to_broadcast([SQ, B, E]), ALU.is_equal))
            link(ve.tensor_tensor(is_second[:, :, :], experts[:, :, :],
                                  top8_f[:, :, 1:2].to_broadcast([SQ, B, E]), ALU.is_equal))
            link(ve.tensor_tensor(chosen[:, :, :], is_first[:, :, :], is_second[:, :, :], ALU.add))
            ve.memset(gate[:, :, 0:1], 1.0)
            link(ve.tensor_tensor(gate[:, :, 1:1 + E], chosen[:, :, :], score[:, :, :], ALU.mult))

            def hidden(s, half):
                u = 2 * s.n + half
                wait_count(ve, s_h_lo, u)
                for m in range(FC):
                    ve.wait_ge(s_sil, FC * u + m + 1)
                    ve.tensor_tensor(hm[:, m, :], up_bank[m][1][:, 0:HALF], sil[:, m, :], ALU.mult).then_inc(s_hm, 1)

            def add_expert(s, half):
                ve.wait_ge(s_dn, 2 * s.n + half + 1)
                for j, b in enumerate(half_batches(half)):
                    y = y_bank[half][j // 2][0:SQ, (j % 2) * D:(j % 2 + 1) * D]
                    ve.wait_ge(s_acc, ACC0 + B * (s.n - 1) + b + 1)
                    ve.scalar_tensor_tensor(x_all[:, b, :], y, gate[:, b, bass.ds(s.n, 1)], x_all[:, b, :],
                                            ALU.mult, ALU.add).then_inc(s_acc, 1)

            hidden(at(0), 0)
            hidden(at(0), 1)
            add_expert(at(0), 0)
            with ve.Fori(0, E // 2) as pair:
                for odd in range(2):
                    s = Step(pair, odd).plus(1)
                    hidden(s, 0)
                    add_expert(s.plus(-1), 1)
                    hidden(s, 1)
                    add_expert(s, 0)
            add_expert(at(E), 1)


_INS = ['x', 'ctx_1024', 'L0_xattn_Wq', 'L0_xattn_bq', 'L0_xattn_Wk', 'L0_xattn_bk', 'L0_xattn_Wv', 'L0_xattn_bv',
        'L0_xattn_Wo', 'L0_xattn_bo', 'L0_ffn_router_w', 'L0_ffn_expert_bias', 'L0_ffn_w1', 'L0_ffn_w2', 'L0_ffn_w3',
        'L0_ffn_sw1', 'L0_ffn_sw2', 'L0_ffn_sw3']


def kernel(**inputs):
    import numpy as _np
    import concourse.bacc as _bacc
    from concourse import mybir as _mybir
    from concourse.bass_utils import run_bass_kernel_spmd as _run

    nc = _bacc.Bacc("TRN2", target_bir_lowering=False, num_devices=1)
    arrays, args = {}, []
    for name in _INS:
        a = _np.ascontiguousarray(inputs[name])
        arrays[f"in_{name}_dram"] = a
        args.append(nc.dram_tensor(f"in_{name}_dram", a.shape, _mybir.dt.from_np(a.dtype), kind="ExternalInput").ap())
    shape = _np.shape(inputs['x'])
    args.append(nc.dram_tensor("out_0_dram", shape, _mybir.dt.float32, kind="ExternalOutput").ap())
    xattn_ffn(nc, *args)
    r = _run(nc, [arrays], core_ids=[0])
    return r.results[0]["out_0_dram"]
```

```python
from contextlib import ExitStack
from typing import Any, NamedTuple

import numpy as np

import concourse.bass as bass
from concourse import mybir

F32 = mybir.dt.float32
F32R = mybir.dt.float32r
BF16 = mybir.dt.bfloat16
I32 = mybir.dt.int32
U32 = mybir.dt.uint32
ACT = mybir.ActivationFunctionType
ALU = mybir.AluOpType
AX_X = mybir.AxisListType.X

P = 128
BANK = 512
EPS = 1e-5

PAIRS = [(0, 0), (0, 1), (1, 0), (1, 1), (0, 2), (2, 0)]
PARTS = 3
PASSES = [(0, 0), (1, 0), (0, 1)]


class Step(NamedTuple):
    pair: Any
    odd: int

    @property
    def n(self):
        return 2 * self.pair + self.odd

    def plus(self, k):
        return Step(self.pair + (self.odd + k) // 2, (self.odd + k) % 2)


def at(n):
    return Step(n // 2, n % 2)


def row(ap, n):
    return ap[bass.ds(n, 1)].rearrange("a r c -> (a r) c")


def wait_count(eng, sem, count):
    if isinstance(count, int) and count <= 0:
        return
    eng.wait_ge(sem, count)


def xattn_ffn(nc, x, ctx_in, wq, bq, wk, bk, wv, bv, wo, bo, router_w, expert_bias,
              w1, w2, w3, sw1, sw2, sw3, out):
    B, SQ, D = x.shape
    SK = ctx_in.shape[1]
    H = 16
    HD = D // H
    E, _, F = w1.shape
    KC = D // P
    FC = F // P
    TC = (SK + P - 1) // P
    SKP = TC * P
    LAST = SK - (TC - 1) * P
    SKE = SK + SK % 2
    HG = 4
    G = H // HG
    GQ = HG * SQ
    STACK = len(PAIRS) * HD
    ROWS = STACK + PARTS
    NT = B * SQ
    HALF = NT // 2
    HB = B // 2
    HM = H // KC
    SCALE = HD ** -0.5
    NW = 3
    S_BANKS = TC

    with ExitStack() as ctx:
        def sb(name, shape, dt=F32):
            return ctx.enter_context(nc.sbuf_tensor(name, shape, dt))

        def sem(name):
            return ctx.enter_context(nc.semaphore(name))

        ident = sb("ident", [P, P])
        identb = sb("identb", [P, P], BF16)
        half_neg = sb("half_neg", [P, B])
        experts = sb("experts", [SQ, B, E])
        experts_i = sb("experts_i", [SQ, B, E], I32)
        wq_sb = sb("wq_sb", [P, KC, D])
        wkv_sb = sb("wkv_sb", [P, 2, KC, D])
        f32r_a = sb("f32r_a", [P, 2 * (2 * KC * D + KC * SKP)], F32R)

        def cut_a(offset, *dims):
            size = 1
            for n in dims:
                size *= n
            v = f32r_a[:, offset:offset + size]
            names = "abc"[:len(dims)]
            return v.rearrange(f"p ({' '.join(names)}) -> p {' '.join(names)}", **dict(zip(names, dims)))

        wkv_part = [cut_a(i * 2 * KC * D, 2, KC, D) for i in range(2)]
        wo_pad = sb("wo_pad", [P, G, D])
        bq_col = sb("bq_col", [P, KC])
        bk_col = sb("bk_col", [P, KC])
        bv_pad = sb("bv_pad", [P, G])
        bo_row = sb("bo_row", [1, D])
        rw_sb = sb("rw_sb", [P, KC, E])
        rw_part = [sb(f"rw_part{i}", [P, KC, E], F32R) for i in range(2)]
        eb_row = sb("eb_row", [SQ, E])
        x_all = sb("x_all", [SQ, B, D])
        stats = sb("stats", [SQ, B, 6])
        mv = sb("mv", [SQ, B, 2])
        var_eps = sb("var_eps", [SQ, B])
        rstd = sb("rstd", [SQ, B])
        xn = sb("xn", [SQ, B, D])
        xnT = sb("xnT", [P, KC, NT])
        qf = sb("qf", [P, KC, NT])
        qr = sb("qr", [P, KC, NT])
        qp = sb("qp", [P, PARTS, KC, NT], BF16)
        qst_all = sb("qst_all", [STACK, H, NT], BF16)
        cx = [sb(f"cx{i}", [P, TC, D]) for i in range(2)]
        ct_part = [cut_a(4 * KC * D + i * KC * SKP, KC, SKP) for i in range(2)]
        kf = sb("kf", [P, KC, SK])
        kr = sb("kr", [P, KC, SK])
        kp = sb("kp", [P, PARTS, KC, SK], BF16)
        kst = [sb(f"kst{i}", [ROWS, H, SKP], BF16) for i in range(2)]
        qst = [sb(f"qst{i}", [ROWS, H, SQ], BF16) for i in range(2)]
        vaug = [sb(f"vaug{i}", [P, TC, H, 2 * HD]) for i in range(2)]
        negm = sb("negm", [SQ, H])
        negm_r = sb("negm_r", [SQ, H])
        mp = sb("mp", [SQ, PARTS, H], BF16)
        mts = sb("mts", [PARTS * H, SQ], BF16)
        probs = [sb(f"probs{i}", [P, TC, GQ]) for i in range(2)]
        den = sb("den", [P, G * SQ])
        ctxn = sb("ctxn", [P, G * SQ])
        xT_part = [sb(f"xT_part{i}", [P, KC, NT], F32R) for i in range(2)]
        logits = sb("logits", [SQ, B, E])
        rowmax = sb("rowmax", [SQ, B])
        ex = sb("ex", [SQ, B, E])
        esum = sb("esum", [SQ, B])
        erec = sb("erec", [SQ, B])
        score = sb("score", [SQ, B, E])
        biased = sb("biased", [SQ, B, E])
        top8 = sb("top8", [SQ, B, 8])
        top8_i = sb("top8_i", [SQ, B, 8], U32)
        top8_f = sb("top8_f", [SQ, B, 8])
        is_first = sb("is_first", [SQ, B, E])
        is_second = sb("is_second", [SQ, B, E])
        chosen = sb("chosen", [SQ, B, E])
        gate = sb("gate", [SQ, B, 1 + E])
        w_raw = [t[:, :, :].rearrange("p c t -> p (c t)")[:, 0:NW * KC * F].rearrange(
            "p (w c n) -> p w c n", w=NW, c=KC) for t in (xnT, qr)]
        w_part = [[sb(f"w_part{i}_{j}", [P, NW, KC, F], F32R) for j in range(2)] for i in range(2)]
        sil, hm = (qf[:, :, :].rearrange("p c t -> p (c t)")[:, i * FC * HALF:(i + 1) * FC * HALF].rearrange(
            "p (m t) -> p m t", m=FC) for i in range(2))
        h_part = [[cut_a((2 * i + j) * FC * HALF, FC, HALF) for j in range(2)] for i in range(2)]

        q_dram = nc.dram_tensor("q_parts", [PARTS, D, NT], BF16, kind="Internal").ap()
        k_dram = [nc.dram_tensor(f"k_parts{i}", [PARTS, D, SK], BF16, kind="Internal").ap() for i in range(2)]

        bank = [ctx.enter_context(nc.psum_tensor(f"bank{i}", [P, BANK], F32)) for i in range(8)]
        s_bank = bank[0:3]
        o_bank = bank[3]
        m_bank = bank[4:6]
        g_bank = bank[6:8]
        up_bank = [bank[0:2], bank[2:4]]
        y_bank = [bank[4:6], bank[6:8]]

        s_ones = sem("ident_base")
        s_ident = sem("ident_ready")
        s_const = sem("consts_ready")
        s_kones = sem("k_stack_ones")
        s_step = sem("shift_chain")
        s_nrm = sem("norm_chain")
        s_apart = sem("wait_apart")
        s_iota = sem("iota_ready")
        d_x = sem("x_in")
        d_wkv = sem("wkv_in")
        d_wq = sem("wq_in")
        d_bias = sem("bias_in")
        d_late = sem("late_consts_in")
        s_wkv_hi = sem("wkv_hi_ready")
        s_wkv_lo = sem("wkv_lo_ready")
        s_vec = sem("vector_chain")
        s_gp = sem("pool_chain")
        s_var = sem("var_ready")
        s_rstd = sem("rstd_ready")
        s_xn = sem("xn_ready")
        s_xt_mm = sem("xn_transposed")
        s_xt = sem("xnT_ready")
        s_q_mm = sem("q_projected")
        s_qf = sem("qf_ready")
        s_qp = sem("q_parts_ready")
        d_q = [sem(f"q_parts_stored{i}") for i in range(2)]
        d_qst = [sem(f"q_stack_in{i}") for i in range(2)]
        d_cx = [sem(f"ctx_in{i}") for i in range(2)]
        s_ct_mm = sem("ctx_transposed")
        s_ct_hi = sem("ctxT_hi_ready")
        s_ct_lo = sem("ctxT_lo_ready")
        s_k_mm = sem("k_projected")
        s_k_ev = sem("k_evacuated")
        s_v_mm = sem("v_projected")
        s_v_ev = sem("v_evacuated")
        s_kp = sem("k_parts_ready")
        d_k = [sem(f"k_parts_stored_m{m}") for m in range(KC)]
        d_kst = [[sem(f"k_stack{i}_in_m{m}") for m in range(KC)] for i in range(2)]
        s_bias_mm = sem("bv_times_wo_done")
        s_bias = sem("output_bias_ready")
        s_qst = sem("q_stack_ready")
        s_m_mm = sem("max_scores_done")
        s_m_rd = sem("max_reduced")
        s_mp = sem("shift_parts_ready")
        s_mt_mm = sem("shift_transposed")
        s_mt_ev = sem("shift_evacuated")
        d_shift = [sem(f"shift_in{i}") for i in range(2)]
        s_s_mm = sem("scores_done")
        s_exp = sem("exp_done")
        s_pv = sem("pv_done")
        s_norm = sem("norm_done")
        s_o_mm = sem("attn_out_done")
        s_o_ev = sem("attn_out_added")
        s_xn2 = sem("xn2_ready")
        s_x2_mm = sem("xn2_transposed")
        s_x2_hi = sem("xn2T_hi_ready")
        s_x2_lo = sem("xn2T_lo_ready")
        s_rw_hi = sem("router_w_hi_ready")
        s_rw_lo = sem("router_w_lo_ready")
        s_lg_mm = sem("logits_done")
        s_lg = sem("logits_shifted")
        s_ex = sem("router_exp_done")
        d_w = [sem(f"w_in{i}") for i in range(2)]
        s_w_hi = sem("w_hi_ready")
        s_w_lo = sem("w_lo_ready")
        s_up = sem("up_done")
        s_sil = sem("silu_done")
        s_hm = sem("hidden_ready")
        s_h_hi = sem("h_hi_ready")
        s_h_lo = sem("h_lo_ready")
        s_dn = sem("down_done")
        s_acc = sem("y_added")
        d_out = sem("out_stored")

        EXP0 = S_BANKS
        PV0 = 2
        O0 = 2
        ACC0 = B

        block = ctx.enter_context(nc.Block())

        def half_batches(half):
            return range(half * HB, half * HB + HB)

        @block.sync
        def _(sp):
            def load_ctx(b):
                wait_count(sp, s_ct_mm, KC * (b.n - 1))
                sp.dma_start(cx[b.odd][:, 0:TC - 1, :], row(ctx_in, b.n)[0:(TC - 1) * P, :].rearrange(
                    "(c p) d -> p c d", p=P)).then_inc(d_cx[b.odd], 16)
                sp.dma_start(cx[b.odd][0:LAST, TC - 1, :], row(ctx_in, b.n)[(TC - 1) * P:SK, :]).then_inc(d_cx[b.odd], 16)

            def stack_k(b):
                for m in range(KC):
                    sp.wait_ge(s_kp, KC * b.n + m + 1)
                    sp.dma_start(k_dram[b.odd][:, m * P:(m + 1) * P, :].rearrange("q p t -> p q t"),
                                 kp[:, :, m, :]).then_inc(d_k[m], 16)
                for m in range(KC):
                    sp.wait_ge(d_k[m], 16 * (b.n + 1))
                    sp.sem_inc(s_apart, 1)
                    if m == 0:
                        wait_count(sp, s_s_mm, G * TC * (b.n - 1))
                        sp.sem_inc(s_apart, 1)
                    for j, (part, _) in enumerate(PAIRS):
                        sp.dma_start(kst[b.odd][j * HD:(j + 1) * HD, m * HM:(m + 1) * HM, 0:SK],
                                     k_dram[b.odd][part, m * P:(m + 1) * P, :].rearrange("(h d) t -> d h t", d=HD)
                                     ).then_inc(d_kst[b.odd][m], 16)

            def stack_q_parts(half):
                cols = slice(half * HALF, (half + 1) * HALF)
                sp.wait_ge(s_qp, half + 1)
                for c in range(KC):
                    sp.dma_start(q_dram[:, c * P:(c + 1) * P, cols].rearrange("q p t -> p q t"),
                                 qp[:, :, c, cols]).then_inc(d_q[half], 16)
                sp.wait_ge(d_q[half], 16 * KC)
                for j, (_, part) in enumerate(PAIRS):
                    sp.dma_start(qst_all[j * HD:(j + 1) * HD, :, cols],
                                 q_dram[part, :, cols].rearrange("(h d) t -> d h t", d=HD)).then_inc(d_qst[half], 16)

            def load_shift(b):
                sp.wait_ge(s_mt_ev, b.n + 1)
                for part in range(PARTS):
                    sp.dma_start(qst[b.odd][STACK + part:STACK + part + 1, :, :],
                                 mts[part * H:(part + 1) * H, :]).then_inc(d_shift[b.odd], 16)

            def load_expert(s, first, second, third):
                wait_count(sp, s_w_lo, s.n - 1)
                for i, w in enumerate((first, second, third)):
                    sp.dma_start(w_raw[s.odd][:, i, :, :], w.rearrange("(c p) n -> p c n", p=P)).then_inc(d_w[s.odd], 16)

            sp.dma_start(x_all[:, :, :], x.rearrange("b q d -> q b d")).then_inc(d_x, 16)
            sp.wait_ge(s_const, 2)
            load_ctx(at(0))
            sp.dma_start(wkv_sb[:, 0, :, :], wk.rearrange("(c p) n -> p c n", p=P)).then_inc(d_wkv, 16)
            sp.dma_start(wkv_sb[:, 1, :, :], wv.rearrange("(c p) n -> p c n", p=P)).then_inc(d_wkv, 16)
            sp.dma_start(wq_sb[:, :, :], wq.rearrange("(c p) n -> p c n", p=P)).then_inc(d_wq, 16)
            sp.dma_start(bq_col[:, :], bq.rearrange("(c p) -> p c", p=P), allow_slow_non_contiguous=True).then_inc(d_bias, 16)
            sp.dma_start(bk_col[:, :], bk.rearrange("(c p) -> p c", p=P), allow_slow_non_contiguous=True).then_inc(d_bias, 16)
            load_ctx(at(1))
            sp.wait_ge(s_const, 6)
            for j in range(HG):
                rows = slice(32 * j + HD, 32 * j + 2 * HD)
                sp.dma_start(wo_pad[rows, :, :],
                             wo.rearrange("(g j d) n -> j d g n", j=HG, d=HD)[j]).then_inc(d_late, 16)
                sp.dma_start(bv_pad[rows, :], bv.rearrange("(g j d) -> j d g", j=HG, d=HD)[j],
                             allow_slow_non_contiguous=True).then_inc(d_late, 16)
            sp.dma_start(bo_row[:, :], bo.rearrange("(a n) -> a n", a=1)).then_inc(d_late, 16)
            sp.dma_start(rw_sb[:, :, :], router_w.rearrange("(c p) e -> p c e", p=P)).then_inc(d_late, 16)
            sp.dma_start(eb_row[:, :], expert_bias.partition_broadcast(SQ)).then_inc(d_late, 16)
            sp.wait_ge(s_kones, 6)
            stack_q_parts(0)
            stack_k(at(0))
            load_ctx(at(2))
            stack_q_parts(1)
            stack_k(at(1))
            load_expert(at(0), sw1, sw3, sw2)
            load_expert(at(1), w1[0], w3[0], w2[0])

            def iteration(i, load=True, stack=True):
                if load:
                    load_ctx(i.plus(3))
                load_shift(i)
                if stack:
                    stack_k(i.plus(2))

            iteration(at(0))
            with sp.Fori(0, B // 2 - 2) as pair:
                iteration(Step(pair, 0).plus(1))
                iteration(Step(pair, 1).plus(1))
            iteration(at(B - 3), load=False)
            iteration(at(B - 2), load=False, stack=False)
            iteration(at(B - 1), load=False, stack=False)

            with sp.Fori(0, E // 2 - 1) as pair:
                for odd in range(2):
                    s = Step(pair, odd).plus(2)
                    e = s.n - 1
                    load_expert(s, row(w1, e), row(w3, e), row(w2, e))
            load_expert(at(E), w1[E - 1], w3[E - 1], w2[E - 1])
            for half in range(2):
                for b in half_batches(half):
                    sp.wait_ge(s_acc, ACC0 + B * E + b + 1)
                    sp.dma_start(out[b], x_all[:, b, :]).then_inc(d_out, 16)
            sp.wait_ge(d_out, 16 * B)

        @block.gpsimd
        def _(gp):
            gp.memset(ident[:, :], 0.0).then_inc(s_ones, 1)
            gp.memset(identb[:, :], 0.0).then_inc(s_ones, 1)
            gp.wait_ge(s_ones, 2)
            for t in (ident, identb):
                gp.affine_select(out=t[:, :], in_=t[:, :], compare_op=ALU.not_equal, fill=1.0, base=0,
                                 pattern=[[-1, P]], channel_multiplier=1).then_inc(s_ident, 1)
            gp.memset(half_neg[:, :], -0.5).then_inc(s_gp, 1)
            pair_of_ones = float(np.array([0x3F803F80], np.uint32).view(np.float32)[0])
            for i in range(2):
                gp.memset(kst[i][:, :, SK:SKP], 0.0).then_inc(s_kones, 1)
            gp.wait_ge(s_kones, 2)
            for i in range(2):
                gp.memset(kst[i][STACK:ROWS, :, SK - 1:SK], 1.0).then_inc(s_kones, 1)
                gp.memset(kst[i][STACK:ROWS, :, 0:SK - 1].bitcast(F32), pair_of_ones).then_inc(s_kones, 1)
            gp.wait_ge(s_kones, 6)
            gp.wait_ge(s_const, 5)
            for i in range(2):
                v = vaug[i][:, TC - 1, :, :].rearrange("p h d -> p (h d)")
                gp.affine_select(out=v, in_=v, compare_op=ALU.is_ge, fill=0.0, base=LAST - 1,
                                 pattern=[[0, 2 * D]], channel_multiplier=-1).then_inc(s_gp, 1)
            gp.wait_ge(s_gp, 3)
            gp.wait_ge(s_var, 1)
            gp.tensor_tensor(rstd[:, :], var_eps[:, :], half_neg[0:SQ, :], ALU.pow).then_inc(s_rstd, 1)
            gp.iota(experts_i[:, :, :], pattern=[[0, B], [1, E]], base=0, channel_multiplier=0).then_inc(s_iota, 1)
            def split_k(b):
                for m in range(KC):
                    n = 2 * (KC * b.n + m) + 3
                    gp.wait_ge(s_k_ev, KC * b.n + m + 1)
                    gp.tensor_tensor(kr[:, m, :], kf[:, m, :], kp[:, 0, m, :], ALU.subtract).then_inc(s_gp, 1)
                    gp.wait_ge(s_gp, n + 1)
                    wait_count(gp, d_k[m], 16 * b.n)
                    gp.sem_inc(s_apart, 1)
                    gp.tensor_copy(kp[:, 1, m, :], kr[:, m, :]).then_inc(s_gp, 1)
                    gp.wait_ge(s_gp, n + 2)
                    gp.tensor_tensor(kp[:, 2, m, :], kr[:, m, :], kp[:, 1, m, :], ALU.subtract).then_inc(s_kp, 1)

            split_k(at(0))
            split_k(at(1))
            with gp.Fori(0, B // 2 - 1) as pair:
                split_k(Step(pair, 0).plus(2))
                split_k(Step(pair, 1).plus(2))

            def cut_weights(s):
                gp.wait_ge(s_w_hi, s.n + 1)
                wait_count(gp, s_dn, 2 * (s.n - 1))
                gp.tensor_tensor(w_part[s.odd][1][:, :, :, :], w_raw[s.odd][:, :, :, :],
                                 w_part[s.odd][0][:, :, :, :].bitcast(F32), ALU.subtract).then_inc(s_w_lo, 1)

            def cut_hidden(s, cut_next=True):
                for half in range(2):
                    if half == 1 and cut_next:
                        cut_weights(s.plus(1))
                    u = 2 * s.n + half
                    gp.wait_ge(s_h_hi, u + 1)
                    wait_count(gp, s_dn, u - 1)
                    gp.tensor_tensor(h_part[half][1][:, :, :], hm[:, :, :],
                                     h_part[half][0][:, :, :].bitcast(F32), ALU.subtract).then_inc(s_h_lo, 1)

            cut_weights(at(0))
            gp.wait_ge(s_var, 2)
            gp.tensor_tensor(rstd[:, :], var_eps[:, :], half_neg[0:SQ, :], ALU.pow).then_inc(s_rstd, 1)
            cut_hidden(at(0))
            with gp.Fori(0, E // 2 - 1) as pair:
                for odd in range(2):
                    cut_hidden(Step(pair, odd).plus(1))
            cut_hidden(at(E - 1))
            cut_hidden(at(E), cut_next=False)

        @block.scalar
        def _(act):
            act.sem_inc(s_exp, EXP0)
            q_bank = [bank[4:6], bank[0:2]]
            act.wait_ge(d_wkv, 32)
            act.activation(wkv_part[0][:, :, :, :], wkv_sb[:, :, :, :], ACT.Copy).then_inc(s_wkv_hi, 1)

            def ctx_hi(b):
                wait_count(act, s_v_mm, 2 * b.n)
                for c in range(KC):
                    act.wait_ge(s_ct_mm, KC * b.n + c + 1)
                    act.activation(ct_part[0][:, c, :], g_bank[c][:, 0:SKP], ACT.Copy).then_inc(s_ct_hi, 1)

            def query(half):
                cols = slice(half * HALF, (half + 1) * HALF)
                for c in range(KC):
                    act.wait_ge(s_xt_mm, KC * half + c + 1)
                    act.activation(xnT[:, c, cols], bank[2 * half + c][:, 0:HALF], ACT.Copy).then_inc(s_xt, 1)
                act.wait_ge(d_bias, 32)
                for m in range(KC):
                    act.wait_ge(s_q_mm, KC * half + m + 1)
                    act.activation(qf[:, m, cols], q_bank[half][m][:, 0:HALF], ACT.Identity, bias=bq_col[:, m:m + 1])
                    act.activation(qp[:, 0, m, cols], q_bank[half][m][:, 0:HALF], ACT.Identity,
                                   bias=bq_col[:, m:m + 1]).then_inc(s_qf, 1)

            def evacuate_k(b, m):
                wait_count(act, s_kp, KC * (b.n - 1) + m + 1)
                wait_count(act, d_k[m], 16 * b.n)
                act.wait_ge(s_k_mm, KC * b.n + m + 1)
                act.activation(kf[:, m, :], g_bank[m][:, 0:SK], ACT.Identity, bias=bk_col[:, m:m + 1])
                act.activation(kp[:, 0, m, :], g_bank[m][:, 0:SK], ACT.Identity,
                               bias=bk_col[:, m:m + 1]).then_inc(s_k_ev, 1)

            def evacuate_v(b):
                wait_count(act, s_pv, G * (b.n - 1) + PV0)
                act.wait_ge(s_v_mm, 2 * b.n + 1)
                act.activation(vaug[b.odd][:, 0:TC - 1, :, HD:2 * HD],
                               g_bank[0][:, 0:(TC - 1) * D].rearrange("p (c h d) -> p c h d", h=H, d=HD),
                               ACT.Copy).then_inc(s_v_ev, 1)
                act.wait_ge(s_v_mm, 2 * b.n + 2)
                act.activation(vaug[b.odd][0:LAST, TC - 1, :, HD:2 * HD],
                               g_bank[1][0:LAST, 0:D].rearrange("p (h d) -> p h d", d=HD),
                               ACT.Copy).then_inc(s_v_ev, 1)

            def stack_q(b):
                wait_count(act, s_s_mm, G * TC * (b.n - 1))
                act.activation(qst[b.odd][0:STACK, :, :],
                               qst_all[:, :, bass.ds(b.n * SQ, SQ)], ACT.Copy).then_inc(s_qst, 1)

            def evacuate_shift(b):
                act.wait_ge(s_mt_mm, b.n + 1)
                if not (isinstance(b.pair, int) and b.n == 0):
                    before = b.plus(-1)
                    act.wait_ge(d_shift[before.odd], 16 * PARTS * (before.pair + 1))
                act.activation(mts[:, :], g_bank[1][0:PARTS * H, 0:SQ // 2].bitcast(BF16), ACT.Copy).then_inc(s_mt_ev, 1)

            def exponentials(b, g):
                act.wait_ge(s_pv, G * b.n + g - 1 + PV0)
                for c in range(TC):
                    act.wait_ge(s_s_mm, TC * (G * b.n + g) + c + 1)
                    act.activation(probs[g % 2][:, c, :], s_bank[c][:, 0:GQ], ACT.Exp, scale=SCALE).then_inc(s_exp, 1)

            def weights_hi(s):
                act.wait_ge(d_w[s.odd], 16 * NW * (s.pair + 1))
                wait_count(act, s_dn, 2 * (s.n - 1))
                act.activation(w_part[s.odd][0][:, :, :, :], w_raw[s.odd][:, :, :, :], ACT.Copy).then_inc(s_w_hi, 1)

            ctx_hi(at(0))
            query(0)
            for m in range(KC):
                evacuate_k(at(0), m)
            act.wait_ge(s_gp, 3)
            evacuate_v(at(0))
            query(1)
            ctx_hi(at(1))
            for m in range(KC):
                evacuate_k(at(1), m)
            act.wait_ge(d_qst[0], 16 * len(PAIRS))
            stack_q(at(0))
            stack_q(at(1))

            def iteration(i, project=True, maxima=True):
                evacuate_shift(i)
                if maxima:
                    evacuate_v(i.plus(1))
                if project:
                    ctx_hi(i.plus(2))
                for g in range(G):
                    exponentials(i, g)
                    if g == 0 and project:
                        for m in range(KC):
                            evacuate_k(i.plus(2), m)
                if project:
                    stack_q(i.plus(2))

            act.wait_ge(d_qst[1], 16 * len(PAIRS))
            iteration(at(0))
            with act.Fori(0, B // 2 - 2) as pair:
                iteration(Step(pair, 0).plus(1))
                iteration(Step(pair, 1).plus(1))
            iteration(at(B - 3))
            weights_hi(at(0))
            act.wait_ge(d_late, 16 * (2 * HG + 3))
            act.activation(rw_part[0][:, :, :], rw_sb[:, :, :], ACT.Copy).then_inc(s_rw_hi, 1)
            iteration(at(B - 2), project=False)
            iteration(at(B - 1), project=False, maxima=False)

            for n in range(2 * KC):
                c, half = n // 2, n % 2
                act.wait_ge(s_x2_mm, n + 1)
                act.activation(xT_part[0][:, c, half * HALF:(half + 1) * HALF], bank[n][:, 0:HALF],
                               ACT.Copy).then_inc(s_x2_hi, 1)
            act.wait_ge(s_lg, 1)
            act.activation(ex[:, :, :], logits[:, :, :], ACT.Exp).then_inc(s_ex, 1)

            def expert(s, cut_next=True):
                for half in range(2):
                    if half == 1 and cut_next:
                        weights_hi(s.plus(1))
                    u = 2 * s.n + half
                    wait_count(act, s_hm, FC * u)
                    for m in range(FC):
                        act.wait_ge(s_up, FC * u + m + 1)
                        act.activation(sil[:, m, :], up_bank[m][0][:, 0:HALF], ACT.Silu).then_inc(s_sil, 1)
                    act.wait_ge(s_hm, FC * (u + 1))
                    wait_count(act, s_dn, u - 1)
                    act.activation(h_part[half][0][:, :, :], hm[:, :, :], ACT.Copy).then_inc(s_h_hi, 1)

            expert(at(0))
            with act.Fori(0, E // 2 - 1) as pair:
                for odd in range(2):
                    expert(Step(pair, odd).plus(1))
            expert(at(E - 1))
            expert(at(E), cut_next=False)

        @block.tensor
        def _(pe):
            def ctx_transposes(b):
                pe.wait_ge(d_cx[b.odd], 32 * (b.pair + 1))
                for c in range(KC):
                    wait_count(pe, s_v_ev, 2 * b.n - 1 + c)
                    for t in range(TC):
                        mm = pe.transpose(g_bank[c][:, t * P:(t + 1) * P], cx[b.odd][:, t, c * P:(c + 1) * P], ident[:, :])
                    mm.then_inc(s_ct_mm, 1)

            def project_k(b, m):
                if m == 0:
                    pe.wait_ge(s_ct_lo, KC * (b.n + 1))
                n = 0
                for c in range(KC):
                    for wi, ci in PASSES:
                        mm = pe.matmul(g_bank[m][:, 0:SKE], wkv_part[wi][:, 0, c, m * P:(m + 1) * P],
                                       ct_part[ci][:, c, 0:SKE], start=(n == 0), stop=(n == KC * len(PASSES) - 1))
                        n += 1
                mm.then_inc(s_k_mm, 1)

            def project_v(b, frees):
                for t in range(TC):
                    if t == 0:
                        pe.wait_ge(*frees[0])
                    if t == TC - 1:
                        pe.wait_ge(*frees[1])
                    dst = g_bank[0][:, t * D:(t + 1) * D] if t < TC - 1 else g_bank[1][:, 0:D]
                    n = 0
                    for c in range(KC):
                        for ci, wi in PASSES:
                            mm = pe.matmul(dst, ct_part[ci][:, c, t * P:(t + 1) * P], wkv_part[wi][:, 1, c, :],
                                           start=(n == 0), stop=(n == KC * len(PASSES) - 1))
                            n += 1
                    if t >= TC - 2:
                        mm.then_inc(s_v_mm, 1)

            def max_scores(b, h):
                wait_count(pe, s_m_rd, H * b.n + h - 1)
                pe.matmul(m_bank[h % 2][0:SQ, 0:SK], qst[b.odd][0:STACK, h, :], kst[b.odd][0:STACK, h, 0:SK],
                          start=True, stop=True).then_inc(s_m_mm, 1)

            def shift_transpose(b):
                pe.wait_ge(s_mp, b.n + 1)
                pe.sem_inc(s_apart, 1)
                pe.transpose(g_bank[1][0:PARTS * H, 0:SQ // 2].bitcast(BF16),
                             mp[:, :, :].rearrange("q s h -> q (s h)"), identb[0:SQ, 0:SQ]).then_inc(s_mt_mm, 1)

            def scores(b, g, c):
                pe.wait_ge(s_exp, TC * (G * b.n + g) + c + 1 - TC + EXP0)
                for j in range(HG):
                    h = HG * g + j
                    mm = pe.matmul(s_bank[c][:, j * SQ:(j + 1) * SQ], kst[b.odd][0:ROWS, h, c * P:(c + 1) * P],
                                   qst[b.odd][0:ROWS, h, :], start=True, stop=True)
                mm.then_inc(s_s_mm, 1)

            def context(b, g):
                for c in range(TC):
                    pe.wait_ge(s_exp, TC * (G * b.n + g) + c + 1 + EXP0)
                    for j in range(HG):
                        mm = pe.matmul(o_bank[32 * j:32 * j + 32, g * SQ:(g + 1) * SQ],
                                       vaug[b.odd][:, c, HG * g + j, :], probs[g % 2][:, c, j * SQ:(j + 1) * SQ],
                                       start=(c == 0), stop=(c == TC - 1))
                mm.then_inc(s_pv, 1)

            def attn_out(b, bank_free):
                pe.wait_ge(s_norm, b.n + 1)
                pe.wait_ge(*bank_free)
                for g in range(G):
                    mm = pe.matmul(g_bank[0][0:SQ, 0:D], ctxn[:, g * SQ:(g + 1) * SQ], wo_pad[:, g, :],
                                   start=(g == 0), stop=(g == G - 1))
                mm.then_inc(s_o_mm, 1)

            pe.sem_inc(s_pv, PV0)
            pe.wait_ge(s_ident, 2)
            q_bank = [bank[4:6], bank[0:2]]

            def query(half):
                pe.wait_ge(s_xn, HB * (half + 1))
                for c in range(KC):
                    for j, b in enumerate(half_batches(half)):
                        mm = pe.transpose(bank[2 * half + c][:, j * SQ:(j + 1) * SQ], xn[:, b, c * P:(c + 1) * P],
                                          ident[0:SQ, 0:SQ])
                    mm.then_inc(s_xt_mm, 1)
                pe.wait_ge(d_wq, 16)
                pe.wait_ge(s_xt, KC * (half + 1))
                for m in range(KC):
                    for c in range(KC):
                        mm = pe.matmul(q_bank[half][m][:, 0:HALF], wq_sb[:, c, m * P:(m + 1) * P],
                                       xnT[:, c, half * HALF:(half + 1) * HALF], start=(c == 0), stop=(c == KC - 1))
                    mm.then_inc(s_q_mm, 1)

            ctx_transposes(at(0))
            query(0)
            pe.wait_ge(s_wkv_lo, 1)
            for m in range(KC):
                project_k(at(0), m)
            project_v(at(0), [(s_k_ev, 1), (s_k_ev, 2)])
            query(1)
            ctx_transposes(at(1))
            for m in range(KC):
                project_k(at(1), m)
            pe.wait_ge(d_late, 16 * (2 * HG + 3))
            for g in range(G):
                mm = pe.matmul(o_bank[0:1, 0:D], bv_pad[:, g:g + 1], wo_pad[:, g, :], start=(g == 0), stop=(g == G - 1))
            mm.then_inc(s_bias_mm, 1)
            pe.wait_ge(s_qf, 2 * KC)
            pe.wait_ge(s_qst, 1)
            for m in range(KC):
                pe.wait_ge(d_kst[0][m], 16 * len(PAIRS))
                for h in range(m * HM, (m + 1) * HM):
                    max_scores(at(0), h)
            pe.wait_ge(s_bias, 1)

            def iteration(i, project=True, maxima=True, before=True):
                pe.wait_ge(s_k_ev, KC * (i.n + 2) if maxima else KC * B)
                if not maxima:
                    pe.wait_ge(s_v_ev, 2 * B)
                shift_transpose(i)
                if before:
                    context(i.plus(-1), G - 1)
                if maxima:
                    project_v(i.plus(1), [(s_o_ev, i.n - 1 + O0), (s_mt_ev, i.n + 1)])
                if project:
                    ctx_transposes(i.plus(2))
                pe.wait_ge(d_shift[i.odd], 16 * PARTS * (i.pair + 1))
                for g in range(G):
                    if maxima and g % (G // KC) == 0:
                        m = g // (G // KC)
                        pe.wait_ge(d_kst[i.plus(1).odd][m], 16 * len(PAIRS) * (i.plus(1).pair + 1))
                        if g == 0:
                            pe.wait_ge(s_qst, i.n + 2)
                    for c in range(TC):
                        scores(i, g, c)
                        if g and maxima:
                            max_scores(i.plus(1), HG * g + c)
                        if g == 1 and c == 0:
                            if before:
                                pe.wait_ge(s_norm, i.n)
                            pe.wait_ge(s_v_ev, 2 * (i.n + 1))
                        if g and c == 0:
                            context(i, g - 1)
                        if g == 2 and c == 0 and before:
                            attn_out(i.plus(-1), (s_k_ev, KC * (i.n + 2) + 1) if project else
                                     (s_v_ev, 2 * B) if maxima else (s_o_ev, B - 2 + O0))
                    if g == 0:
                        if project:
                            project_k(i.plus(2), 0)
                        for h in range(HG if maxima else 0):
                            max_scores(i.plus(1), h)
                            if h == 1 and project:
                                project_k(i.plus(2), 1)
                    elif maxima:
                        max_scores(i.plus(1), HG * g + TC)

            iteration(at(0), before=False)
            with pe.Fori(0, B // 2 - 2) as pair:
                iteration(Step(pair, 0).plus(1))
                iteration(Step(pair, 1).plus(1))
            iteration(at(B - 3))
            iteration(at(B - 2), project=False)
            iteration(at(B - 1), project=False, maxima=False)
            context(at(B - 1), G - 1)
            attn_out(at(B - 1), (s_o_ev, B - 1 + O0))

            pe.wait_ge(s_exp, TC * G * B + EXP0)
            pe.wait_ge(s_norm, B)
            for n in range(2 * KC):
                c, half = n // 2, n % 2
                pe.wait_ge(s_xn2, B)
                for j, b in enumerate(half_batches(half)):
                    mm = pe.transpose(bank[n][:, j * SQ:(j + 1) * SQ], xn[:, b, c * P:(c + 1) * P], ident[0:SQ, 0:SQ])
                mm.then_inc(s_x2_mm, 1)
            pe.wait_ge(s_x2_lo, 2 * KC)
            pe.wait_ge(s_m_rd, H * B)
            pe.wait_ge(s_rw_lo, 1)

            def logits():
                for b in range(B):
                    n = 0
                    for c in range(KC):
                        for xi, wi in PASSES:
                            mm = pe.matmul(m_bank[0][0:SQ, b * E:(b + 1) * E], xT_part[xi][:, c, b * SQ:(b + 1) * SQ],
                                           rw_part[wi][:, c, :], start=(n == 0), stop=(n == KC * len(PASSES) - 1))
                            n += 1
                mm.then_inc(s_lg_mm, 1)

            def up(s, half):
                u = 2 * s.n + half
                if half == 0:
                    pe.wait_ge(s_w_lo, s.n + 1)
                for m in range(FC):
                    wait_count(pe, s_hm, FC * (u - 1) + m + 1)
                    for w in range(2):
                        n = 0
                        for c in range(KC):
                            for wi, xi in PASSES:
                                mm = pe.matmul(up_bank[m][w][:, 0:HALF], w_part[s.odd][wi][:, w, c, m * P:(m + 1) * P],
                                               xT_part[xi][:, c, half * HALF:(half + 1) * HALF],
                                               start=(n == 0), stop=(n == KC * len(PASSES) - 1))
                                n += 1
                    mm.then_inc(s_up, 1)

            def down(s, half):
                u = 2 * s.n + half
                pe.wait_ge(s_h_lo, u + 1)
                pe.wait_ge(s_acc, ACC0 + B * (s.n - 1) + HB * (half + 1))
                for j in range(HB):
                    n = 0
                    for c in range(FC):
                        for hi, wi in PASSES:
                            mm = pe.matmul(y_bank[half][j // 2][0:SQ, (j % 2) * D:(j % 2 + 1) * D],
                                           h_part[half][hi][:, c, j * SQ:(j + 1) * SQ], w_part[s.odd][wi][:, 2, c, :],
                                           start=(n == 0), stop=(n == FC * len(PASSES) - 1))
                            n += 1
                mm.then_inc(s_dn, 1)

            up(at(0), 0)
            logits()
            up(at(0), 1)
            pe.wait_ge(s_lg, 1)
            pe.wait_ge(s_o_ev, B + O0)
            down(at(0), 0)
            with pe.Fori(0, E // 2) as pair:
                for odd in range(2):
                    s = Step(pair, odd).plus(1)
                    up(s, 0)
                    down(s.plus(-1), 1)
                    up(s, 1)
                    down(s, 0)
            down(at(E), 1)

        @block.vector
        def _(ve):
            chain = [0]

            def link(ins):
                chain[0] += 1
                ins.then_inc(s_vec, 1)
                ve.wait_ge(s_vec, chain[0])

            ve.sem_inc(s_o_ev, O0)
            for i in range(2):
                ve.memset(cx[i][:, TC - 1, :], 0.0).then_inc(s_const, 1)
            ve.memset(bv_pad[:, :], 0.0).then_inc(s_const, 1)
            for i in range(2):
                ve.memset(vaug[i][:, :, :, :], 1.0).then_inc(s_const, 1)
            ve.memset(wo_pad[:, :, :], 0.0).then_inc(s_const, 1)

            def row_stats(b):
                r = x_all[:, bass.ds(b, 1), :].rearrange("q a d -> q (a d)")
                return ve.bn_stats(stats[:, bass.ds(b, 1), :].rearrange("q a s -> q (a s)"), r)

            def var_and_eps():
                for b in range(B - 1):
                    ve.bn_aggr(mv[:, b, :], stats[:, b, :])
                link(ve.bn_aggr(mv[:, B - 1, :], stats[:, B - 1, :]))
                ve.tensor_scalar(var_eps[:, :], mv[:, :, 1], EPS, None, ALU.add).then_inc(s_var, 1)

            def normalise_x(ready, round_):
                ve.wait_ge(s_rstd, round_)
                for b in range(B):
                    ve.tensor_scalar(xn[:, b, :], x_all[:, b, :], mv[:, b, 0:1], rstd[:, b:b + 1],
                                     ALU.subtract, ALU.mult).then_inc(ready, 1)

            def cut_query(half):
                cols = slice(half * HALF, (half + 1) * HALF)
                ve.wait_ge(s_qf, KC * (half + 1))
                link(ve.tensor_tensor(qr[:, :, cols], qf[:, :, cols], qp[:, 0, :, cols], ALU.subtract))
                link(ve.tensor_copy(qp[:, 1, :, cols], qr[:, :, cols]))
                ve.tensor_tensor(qp[:, 2, :, cols], qr[:, :, cols], qp[:, 1, :, cols], ALU.subtract).then_inc(s_qp, 1)

            def ctx_lo(b):
                for c in range(KC):
                    ve.wait_ge(s_ct_hi, KC * b.n + c + 1)
                    ve.tensor_tensor(ct_part[1][:, c, :], g_bank[c][:, 0:SKP],
                                     ct_part[0][:, c, :].bitcast(F32), ALU.subtract).then_inc(s_ct_lo, 1)

            def reduce_max(b, h):
                ve.wait_ge(s_m_mm, H * b.n + h + 1)
                ve.tensor_reduce(negm[:, h:h + 1], m_bank[h % 2][0:SQ, 0:SK], AX_X, ALU.max,
                                 negate=True).then_inc(s_m_rd, 1)

            def cut_shift(b):
                n = 3 * b.n
                ve.wait_ge(s_m_rd, H * (b.n + 1))
                wait_count(ve, s_mt_mm, b.n)
                ve.tensor_copy(mp[:, 0, :], negm[:, :]).then_inc(s_step, 1)
                ve.wait_ge(s_step, n + 1)
                ve.tensor_tensor(negm_r[:, :], negm[:, :], mp[:, 0, :], ALU.subtract).then_inc(s_step, 1)
                ve.wait_ge(s_step, n + 2)
                ve.tensor_copy(mp[:, 1, :], negm_r[:, :]).then_inc(s_step, 1)
                ve.wait_ge(s_step, n + 3)
                ve.tensor_tensor(mp[:, 2, :], negm_r[:, :], mp[:, 1, :], ALU.subtract).then_inc(s_mp, 1)

            def denominators(b, half):
                n = 2 * b.n
                if half == 0:
                    ve.wait_ge(s_pv, G * (b.n + 1) + PV0)
                    ve.sem_inc(s_apart, 1)
                    ve.stream_shuffle(den[:, :], o_bank[:, 0:G * SQ],
                                      [i % HD for i in range(32)]).then_inc(s_nrm, 1)
                    ve.wait_ge(s_nrm, n + 1)
                cols = slice(half * G * SQ // 2, (half + 1) * G * SQ // 2)
                ins = ve.reciprocal(den[:, cols], den[:, cols])
                if half:
                    ins.then_inc(s_nrm, 1)

            def normalise(b):
                ve.wait_ge(s_nrm, 2 * b.n + 2)
                wait_count(ve, s_o_mm, b.n)
                ve.tensor_tensor(ctxn[:, :], o_bank[:, 0:G * SQ], den[:, :], ALU.mult).then_inc(s_norm, 1)

            def add_attn_out(b):
                ve.wait_ge(s_o_mm, b.n + 1)
                row = x_all[:, bass.ds(b.n, 1), :].rearrange("q a d -> q (a d)")
                ve.tensor_tensor(row, g_bank[0][0:SQ, 0:D], row, ALU.add).then_inc(s_o_ev, 1)

            ve.wait_ge(d_x, 16)
            for b in range(B - 1):
                row_stats(b)
            link(row_stats(B - 1))
            var_and_eps()
            ve.wait_ge(s_wkv_hi, 1)
            ve.tensor_tensor(wkv_part[1][:, :, :, :], wkv_sb[:, :, :, :], wkv_part[0][:, :, :, :].bitcast(F32),
                             ALU.subtract).then_inc(s_wkv_lo, 1)
            ctx_lo(at(0))
            normalise_x(s_xn, 1)
            cut_query(0)
            cut_query(1)
            ctx_lo(at(1))
            ve.wait_ge(s_bias_mm, 1)
            ve.tensor_tensor(wo_pad[0:1, 0, :], o_bank[0:1, 0:D], bo_row[:, :], ALU.add).then_inc(s_bias, 1)
            for h in range(H):
                reduce_max(at(0), h)
            cut_shift(at(0))

            def iteration(i, project=True, maxima=True, before=True):
                if before:
                    denominators(i.plus(-1), 0)
                if project:
                    ctx_lo(i.plus(2))
                if before:
                    denominators(i.plus(-1), 1)
                    normalise(i.plus(-1))
                for h in range(H if maxima else 0):
                    reduce_max(i.plus(1), h)
                    if before and h == 9:
                        add_attn_out(i.plus(-1))
                if maxima:
                    cut_shift(i.plus(1))

            iteration(at(0), before=False)
            with ve.Fori(0, B // 2 - 2) as pair:
                iteration(Step(pair, 0).plus(1))
                iteration(Step(pair, 1).plus(1))
            iteration(at(B - 3))
            iteration(at(B - 2), project=False)
            iteration(at(B - 1), project=False, maxima=False)
            add_attn_out(at(B - 2))
            ve.wait_ge(d_late, 16 * (2 * HG + 3))
            ve.wait_ge(s_rw_hi, 1)
            ve.tensor_tensor(rw_part[1][:, :, :], rw_sb[:, :, :], rw_part[0][:, :, :].bitcast(F32),
                             ALU.subtract).then_inc(s_rw_lo, 1)
            ve.wait_ge(s_iota, 1)
            link(ve.tensor_copy(experts[:, :, :], experts_i[:, :, :]))
            ve.wait_ge(s_o_ev, B - 1 + O0)
            for b in range(B - 1):
                row_stats(b)
            denominators(at(B - 1), 0)
            denominators(at(B - 1), 1)
            normalise(at(B - 1))
            add_attn_out(at(B - 1))
            ve.wait_ge(s_o_ev, B + O0)
            ve.sem_inc(s_acc, ACC0)
            link(row_stats(B - 1))
            var_and_eps()
            normalise_x(s_xn2, 2)
            for n in range(2 * KC):
                c, half = n // 2, n % 2
                cols = slice(half * HALF, (half + 1) * HALF)
                ve.wait_ge(s_x2_hi, n + 1)
                ve.tensor_tensor(xT_part[1][:, c, cols], bank[n][:, 0:HALF], xT_part[0][:, c, cols].bitcast(F32),
                                 ALU.subtract).then_inc(s_x2_lo, 1)

            def wide(t):
                return t.unsqueeze(2).to_broadcast([SQ, B, E])

            ve.wait_ge(s_lg_mm, 1)
            lg = m_bank[0][0:SQ, 0:B * E].rearrange("q (b e) -> q b e", e=E)
            link(ve.tensor_reduce(rowmax[:, :], lg, AX_X, ALU.max))
            ve.tensor_tensor(logits[:, :, :], lg, wide(rowmax[:, :]), ALU.subtract).then_inc(s_lg, 1)
            ve.wait_ge(s_ex, 1)
            link(ve.tensor_reduce(esum[:, :], ex[:, :, :], AX_X, ALU.add))
            link(ve.reciprocal(erec[:, :], esum[:, :]))
            link(ve.tensor_tensor(score[:, :, :], ex[:, :, :], wide(erec[:, :]), ALU.mult))
            link(ve.tensor_tensor(biased[:, :, :], score[:, :, :], eb_row[:, :].unsqueeze(1).to_broadcast([SQ, B, E]), ALU.add))
            for b in range(B - 1):
                ve.max(top8[:, b, :], biased[:, b, :])
            link(ve.max(top8[:, B - 1, :], biased[:, B - 1, :]))
            for b in range(B - 1):
                ve.max_index(top8_i[:, b, :], top8[:, b, :], biased[:, b, :])
            link(ve.max_index(top8_i[:, B - 1, :], top8[:, B - 1, :], biased[:, B - 1, :]))
            link(ve.tensor_copy(top8_f[:, :, :], top8_i[:, :, :]))
            link(ve.tensor_tensor(is_first[:, :, :], experts[:, :, :],
                                  top8_f[:, :, 0:1].to_broadcast([SQ, B, E]), ALU.is_equal))
            link(ve.tensor_tensor(is_second[:, :, :], experts[:, :, :],
                                  top8_f[:, :, 1:2].to_broadcast([SQ, B, E]), ALU.is_equal))
            link(ve.tensor_tensor(chosen[:, :, :], is_first[:, :, :], is_second[:, :, :], ALU.add))
            ve.memset(gate[:, :, 0:1], 1.0)
            link(ve.tensor_tensor(gate[:, :, 1:1 + E], chosen[:, :, :], score[:, :, :], ALU.mult))

            def hidden(s, half):
                u = 2 * s.n + half
                wait_count(ve, s_h_lo, u)
                for m in range(FC):
                    ve.wait_ge(s_sil, FC * u + m + 1)
                    ve.tensor_tensor(hm[:, m, :], up_bank[m][1][:, 0:HALF], sil[:, m, :], ALU.mult).then_inc(s_hm, 1)

            def add_expert(s, half):
                ve.wait_ge(s_dn, 2 * s.n + half + 1)
                for j, b in enumerate(half_batches(half)):
                    y = y_bank[half][j // 2][0:SQ, (j % 2) * D:(j % 2 + 1) * D]
                    ve.wait_ge(s_acc, ACC0 + B * (s.n - 1) + b + 1)
                    ve.scalar_tensor_tensor(x_all[:, b, :], y, gate[:, b, bass.ds(s.n, 1)], x_all[:, b, :],
                                            ALU.mult, ALU.add).then_inc(s_acc, 1)

            hidden(at(0), 0)
            hidden(at(0), 1)
            add_expert(at(0), 0)
            with ve.Fori(0, E // 2) as pair:
                for odd in range(2):
                    s = Step(pair, odd).plus(1)
                    hidden(s, 0)
                    add_expert(s.plus(-1), 1)
                    hidden(s, 1)
                    add_expert(s, 0)
            add_expert(at(E), 1)


_INS = ['x', 'ctx_1024', 'L0_xattn_Wq', 'L0_xattn_bq', 'L0_xattn_Wk', 'L0_xattn_bk', 'L0_xattn_Wv', 'L0_xattn_bv',
        'L0_xattn_Wo', 'L0_xattn_bo', 'L0_ffn_router_w', 'L0_ffn_expert_bias', 'L0_ffn_w1', 'L0_ffn_w2', 'L0_ffn_w3',
        'L0_ffn_sw1', 'L0_ffn_sw2', 'L0_ffn_sw3']


def kernel(**inputs):
    import numpy as _np
    import concourse.bacc as _bacc
    from concourse import mybir as _mybir
    from concourse.bass_utils import run_bass_kernel_spmd as _run

    nc = _bacc.Bacc("TRN2", target_bir_lowering=False, num_devices=1)
    arrays, args = {}, []
    for name in _INS:
        a = _np.ascontiguousarray(inputs[name])
        arrays[f"in_{name}_dram"] = a
        args.append(nc.dram_tensor(f"in_{name}_dram", a.shape, _mybir.dt.from_np(a.dtype), kind="ExternalInput").ap())
    shape = _np.shape(inputs['x'])
    args.append(nc.dram_tensor("out_0_dram", shape, _mybir.dt.float32, kind="ExternalOutput").ap())
    xattn_ffn(nc, *args)
    r = _run(nc, [arrays], core_ids=[0])
    return r.results[0]["out_0_dram"]
```

```python
from contextlib import ExitStack
from typing import Any, NamedTuple

import numpy as np

import concourse.bass as bass
from concourse import mybir

F32 = mybir.dt.float32
F32R = mybir.dt.float32r
BF16 = mybir.dt.bfloat16
I32 = mybir.dt.int32
U32 = mybir.dt.uint32
ACT = mybir.ActivationFunctionType
ALU = mybir.AluOpType
AX_X = mybir.AxisListType.X

P = 128
BANK = 512
EPS = 1e-5

PARTS = 3
RUNS = [(0, 3), (1, 3), (2, 1)]
PASSES = [(0, 0), (1, 0), (0, 1)]


class Step(NamedTuple):
    pair: Any
    odd: int

    @property
    def n(self):
        return 2 * self.pair + self.odd

    def plus(self, k):
        return Step(self.pair + (self.odd + k) // 2, (self.odd + k) % 2)


def at(n):
    return Step(n // 2, n % 2)


def row(ap, n):
    return ap[bass.ds(n, 1)].rearrange("a r c -> (a r) c")


def row_of(ap, n):
    return ap[bass.ds(n, 1)].rearrange("a c -> (a c)")


def wait_count(eng, sem, count):
    if isinstance(count, int) and count <= 0:
        return
    eng.wait_ge(sem, count)


def xattn_ffn(nc, x, ctx_in, wq, bq, wk, bk, wv, bv, wo, bo, router_w, expert_bias,
              w1, w2, w3, sw1, sw2, sw3, out):
    B, SQ, D = x.shape
    SK = ctx_in.shape[1]
    H = 16
    HD = D // H
    E, _, F = w1.shape
    KC = D // P
    FC = F // P
    TC = (SK + P - 1) // P
    SKP = TC * P
    LAST = SK - (TC - 1) * P
    SKE = SK + SK % 2
    HG = 4
    G = H // HG
    GQ = HG * SQ
    STACK = sum(k for _, k in RUNS) * HD
    ROWS = STACK + PARTS
    ONES = STACK // 32 * 32
    NT = B * SQ
    HALF = NT // 2
    HB = B // 2
    HM = H // KC
    SCALE = HD ** -0.5
    NW = 3
    S_BANKS = TC

    with ExitStack() as ctx:
        def sb(name, shape, dt=F32):
            return ctx.enter_context(nc.sbuf_tensor(name, shape, dt))

        def sem(name):
            return ctx.enter_context(nc.semaphore(name))

        ident = sb("ident", [P, P])
        identb = sb("identb", [P, P], BF16)
        half_neg = sb("half_neg", [P, B])
        experts = sb("experts", [SQ, B, E])
        experts_i = sb("experts_i", [SQ, B, E], I32)
        wq_sb = sb("wq_sb", [P, KC, D])
        wkv_sb = sb("wkv_sb", [P, 2, KC, D])
        f32r_a = sb("f32r_a", [P, 2 * (2 * KC * D + KC * SKP)], F32R)

        def cut_a(offset, *dims):
            size = 1
            for n in dims:
                size *= n
            v = f32r_a[:, offset:offset + size]
            names = "abc"[:len(dims)]
            return v.rearrange(f"p ({' '.join(names)}) -> p {' '.join(names)}", **dict(zip(names, dims)))

        wkv_part = [cut_a(i * 2 * KC * D, 2, KC, D) for i in range(2)]
        wo_sb = sb("wo_sb", [P, KC, D])
        bq_col = sb("bq_col", [P, KC])
        bk_col = sb("bk_col", [P, KC])
        bv_col = sb("bv_col", [P, KC])
        bv_wide = sb("bv_wide", [P, KC, SQ])
        bo_rows = sb("bo_rows", [SQ, D])
        out_bias = sb("out_bias", [SQ, D])
        rw_sb = sb("rw_sb", [P, KC, E])
        rw_part = [sb(f"rw_part{i}", [P, KC, E], F32R) for i in range(2)]
        eb_row = sb("eb_row", [SQ, E])
        x_all = sb("x_all", [SQ, B, D])
        stats = sb("stats", [SQ, B, 6])
        mv = sb("mv", [SQ, B, 2])
        var_eps = sb("var_eps", [SQ, B])
        rstd = sb("rstd", [SQ, B])
        xn = sb("xn", [SQ, B, D])
        xnT = sb("xnT", [P, KC, NT])
        qf = sb("qf", [P, KC, NT])
        qr = sb("qr", [P, KC, NT])
        qp = sb("qp", [P, PARTS, KC, NT], BF16)
        qst_or_gates = sb("qst_or_gates", [P, H * NT], BF16)
        qst_all = qst_or_gates[0:STACK, :].rearrange("p (h t) -> p h t", h=H)
        gates = qst_or_gates[:, 0:2 * E * NT].bitcast(F32).rearrange("p (e t) -> p e t", e=E)
        cx = [sb(f"cx{i}", [P, TC, D]) for i in range(2)]
        kf = sb("kf", [P, KC, SK])
        kr = sb("kr", [P, KC, SK])
        kp = sb("kp", [P, KC, PARTS, SK], BF16)
        kst = [sb(f"kst{i}", [ROWS, H, SKP], BF16) for i in range(2)]
        qst = [sb(f"qst{i}", [ROWS, H, SQ], BF16) for i in range(2)]
        vaug = [sb(f"vaug{i}", [P, TC, H, 2 * HD]) for i in range(2)]
        negm = sb("negm", [SQ, H])
        negm_r = sb("negm_r", [SQ, H])
        mp = [sb(f"mp{i}", [SQ, PARTS, HM], BF16) for i in range(2)]
        mts = [sb(f"mts{i}", [PARTS * HM, SQ], BF16) for i in range(2)]
        probs = [sb(f"probs{i}", [P, TC, GQ]) for i in range(2)]
        sums = sb("sums", [P, G * SQ])
        rden = sb("rden", [SQ, H])
        heads_q = sb("heads_q", [SQ, H, HD])
        headsT = sb("headsT", [P, KC, SQ])
        xT_part = [sb(f"xT_part{i}", [P, KC, NT], F32R) for i in range(2)]
        logits = sb("logits", [SQ, B, E])
        rowmax = sb("rowmax", [SQ, B])
        ex = sb("ex", [SQ, B, E])
        esum = sb("esum", [SQ, B])
        erec = sb("erec", [SQ, B])
        score = sb("score", [SQ, B, E])
        biased = sb("biased", [SQ, B, E])
        top8 = sb("top8", [SQ, B, 8])
        top8_i = sb("top8_i", [SQ, B, 8], U32)
        top8_f = sb("top8_f", [SQ, B, 8])
        is_first = sb("is_first", [SQ, B, E])
        is_second = sb("is_second", [SQ, B, E])
        chosen = sb("chosen", [SQ, B, E])
        gate = sb("gate", [SQ, B, E])
        w_raw = [t[:, :, :].rearrange("p c t -> p (c t)")[:, 0:NW * KC * F].rearrange(
            "p (w c n) -> p w c n", w=NW, c=KC) for t in (xnT, qr)]
        w_part = [[sb(f"w_part{i}_{j}", [P, NW, KC, F], F32R) for j in range(2)] for i in range(2)]
        sil, hm = (qf[:, :, :].rearrange("p c t -> p (c t)")[:, i * FC * HALF:(i + 1) * FC * HALF].rearrange(
            "p (m t) -> p m t", m=FC) for i in range(2))
        h_part = [[cut_a((2 * i + j) * FC * HALF, FC, HALF) for j in range(2)] for i in range(2)]

        logitsT = gateT = probs[0][:, :, :].rearrange("p c t -> p (c t)")[0:E, 0:NT]
        gated, y_sb = ([probs[i][:, :, :].rearrange("p c t -> p (c t)")[:, 0:FC * HALF].rearrange(
            "p (m t) -> p m t", m=FC) for i in order] for order in ([1], [0, 1]))
        gated = gated[0]
        odd_ct = w_part[1][0][:, :, :, :].rearrange("p w c n -> p (w c n)")[:, 0:2 * KC * SKP].rearrange(
            "p (i c t) -> p i c t", i=2, c=KC)
        ct_part = [[cut_a(4 * KC * D + i * KC * SKP, KC, SKP) for i in range(2)], [odd_ct[:, i] for i in range(2)]]

        q_dram = nc.dram_tensor("q_parts", [PARTS, D, NT], BF16, kind="Internal").ap()
        gate_dram = nc.dram_tensor("gates", [E, NT], F32, kind="Internal").ap()
        k_dram = [nc.dram_tensor(f"k_parts{i}", [KC, HM, HD, PARTS, SK], BF16, kind="Internal").ap() for i in range(2)]

        bank = [ctx.enter_context(nc.psum_tensor(f"bank{i}", [P, BANK], F32)) for i in range(8)]
        s_bank = bank[0:3]
        o_bank = bank[3]
        m_bank = bank[4:6]
        MID = range(5, 13)
        max_banks = [4 + h % 2 for h in range(MID.start)]
        max_banks += [(5, 7, 4)[(h - MID.start) % 3] for h in MID]
        max_banks += [4 + (h - MID.stop) % 2 for h in range(MID.stop, H)]
        first_max_banks = [(4, 5, 1, 2)[h % 4] for h in range(H)]
        mt_bank = [bank[3][0:PARTS * HM, G * SQ:G * SQ + SQ // 2].bitcast(BF16),
                   bank[0][0:PARTS * HM, 0:SQ // 2].bitcast(BF16)]
        g_bank = bank[6:8]
        logits_bank = [bank[7], bank[4]]
        up_bank = [bank[0:2], bank[2:4]]
        y_bank = [bank[4:6], bank[6:8]]

        s_ones = sem("ident_base")
        s_ident = sem("ident_ready")
        s_const = sem("consts_ready")
        s_kones = sem("k_stack_ones")
        s_step = sem("shift_chain")
        s_nrm = sem("norm_chain")
        s_apart = sem("wait_apart")
        s_iota = sem("iota_ready")
        d_x = sem("x_in")
        d_wkv = [sem("wk_in"), sem("wv_in")]
        d_wq = sem("wq_in")
        d_bias = sem("bias_in")
        d_late = sem("late_consts_in")
        s_wkv_hi = sem("wkv_hi_ready")
        s_wkv_lo = sem("wkv_lo_ready")
        s_vec = sem("vector_chain")
        s_gp = sem("pool_chain")
        s_var = sem("var_ready")
        s_rstd = sem("rstd_ready")
        s_xn = sem("xn_ready")
        s_xt_mm = sem("xn_transposed")
        s_xt = sem("xnT_ready")
        s_q_mm = sem("q_projected")
        s_qf = sem("qf_ready")
        s_qp = sem("q_parts_ready")
        d_q = [sem(f"q_parts_stored{i}") for i in range(2)]
        d_qst = [sem(f"q_stack_in{i}") for i in range(2)]
        d_cx = [sem(f"ctx_in{i}") for i in range(2)]
        s_ct_mm = sem("ctx_transposed")
        s_ct_hi = sem("ctxT_hi_ready")
        s_ct_lo = sem("ctxT_lo_ready")
        s_k_mm = sem("k_projected")
        s_k_ev = sem("k_evacuated")
        s_v_mm = sem("v_projected")
        s_v_ev = sem("v_evacuated")
        s_kp = sem("k_parts_ready")
        d_k = [sem(f"k_parts_stored_m{m}") for m in range(KC)]
        d_kst = [[sem(f"k_stack{i}_in_m{m}") for m in range(KC)] for i in range(2)]
        s_bv = sem("bv_spread")
        s_bias_mm = sem("bv_times_wo_done")
        s_bias = sem("output_bias_ready")
        s_qst = sem("q_stack_ready")
        s_m_mm = sem("max_scores_done")
        s_m_rd = sem("max_reduced")
        s_mp = sem("shift_parts_ready")
        s_mt_mm = sem("shift_transposed")
        s_mt_ev = sem("shift_evacuated")
        d_shift = [[sem(f"shift{i}_in_m{m}") for m in range(KC)] for i in range(2)]
        s_s_mm = sem("scores_done")
        s_exp = sem("exp_done")
        s_pv = sem("pv_done")
        s_sums = sem("sums_evacuated")
        s_sums_mm = sem("sums_transposed")
        s_norm = sem("heads_normalised")
        s_ht_mm = sem("heads_transposed")
        s_ht = sem("headsT_ready")
        s_o_mm = sem("attn_out_done")
        s_o_ev = sem("attn_out_added")
        s_xn2 = sem("xn2_ready")
        s_x2_mm = sem("xn2_transposed")
        s_x2_hi = sem("xn2T_hi_ready")
        s_x2_lo = sem("xn2T_lo_ready")
        s_rw_hi = sem("router_w_hi_ready")
        s_rw_lo = sem("router_w_lo_ready")
        s_lt_mm = sem("logitsT_done")
        s_lt = sem("logitsT_ready")
        s_lg_mm = sem("logits_done")
        s_lg = sem("logits_shifted")
        s_ex = sem("router_exp_done")
        d_w = [sem(f"w_in{i}") for i in range(2)]
        s_w_hi = sem("w_hi_ready")
        s_w_lo = sem("w_lo_ready")
        s_w2_lo = sem("w2_lo_ready")
        s_up = sem("up_done")
        s_sil = sem("silu_done")
        s_hm = sem("hidden_ready")
        s_h_hi = sem("h_hi_ready")
        s_h_lo = sem("h_lo_ready")
        s_dn = sem("down_done")
        s_gate = sem("gates_ready")
        s_gt_mm = sem("gates_transposed")
        s_gt = sem("gatesT_ready")
        d_gt = [sem(f"gates_stored{i}") for i in range(2)]
        d_gate_rest = sem("first_gates_rest_in")
        d_gate = [sem(f"gates_in{i}") for i in range(2)]
        s_gated = sem("w3_product_gated")
        s_y = sem("y_evacuated")
        s_yt_mm = sem("y_transposed")
        s_acc = sem("y_added")
        d_out = sem("out_stored")

        LATE = 5
        def chunk_order(g):
            return [1, 2, 0] if g % G == 0 else [0, 1, 2]

        LN2 = [range(HB), range(HB, B - 1), range(B - 1, B)]

        EXP0 = S_BANKS
        PV0 = 2
        O0 = 2
        W0 = 2

        block = ctx.enter_context(nc.Block())

        def half_batches(half):
            return range(half * HB, half * HB + HB)

        @block.sync
        def _(sp):
            def load_ctx(b):
                wait_count(sp, s_ct_mm, KC * (b.n - 1))
                sp.dma_start(cx[b.odd][:, 0:TC - 1, :], row(ctx_in, b.n)[0:(TC - 1) * P, :].rearrange(
                    "(c p) d -> p c d", p=P)).then_inc(d_cx[b.odd], 16)
                sp.dma_start(cx[b.odd][0:LAST, TC - 1, :], row(ctx_in, b.n)[(TC - 1) * P:SK, :]).then_inc(d_cx[b.odd], 16)

            def store_k(b, m):
                sp.wait_ge(s_kp, KC * b.n + m + 1)
                sp.dma_start(k_dram[b.odd][m].rearrange("h d k t -> (h d) k t"), kp[:, m, :, :]).then_inc(d_k[m], 16)

            def stack_k(b, m):
                sp.wait_ge(d_k[m], 16 * (b.n + 1))
                sp.sem_inc(s_apart, 1)
                if not (isinstance(b.pair, int) and b.n < 2):
                    sp.wait_ge(s_s_mm, TC * (G * (b.n - 2) + G // KC * (m + 1)))
                    sp.sem_inc(s_apart, 1)
                first = 0
                for _, parts in RUNS:
                    sp.dma_start(kst[b.odd][first:first + parts * HD, m * HM:(m + 1) * HM, 0:SK],
                                 k_dram[b.odd][m][:, :, 0:parts, :].rearrange("h d k t -> (d k) h t")
                                 ).then_inc(d_kst[b.odd][m], 16)
                    first += parts * HD

            def store_q(half, m):
                cols = slice(half * HALF, (half + 1) * HALF)
                sp.wait_ge(s_qp, KC * half + m + 1)
                sp.dma_start(q_dram[:, m * P:(m + 1) * P, cols].rearrange("q p t -> p q t"),
                             qp[:, :, m, cols]).then_inc(d_q[half], 16)

            def stack_q_parts(half):
                cols = slice(half * HALF, (half + 1) * HALF)
                sp.wait_ge(d_q[half], 16 * KC)
                first = 0
                for part, copies in RUNS:
                    for k in range(copies):
                        sp.dma_start(qst_all[first + k:first + copies * HD:copies, :, cols],
                                     q_dram[part, :, cols].rearrange("(h d) t -> d h t", d=HD)).then_inc(d_qst[half], 16)
                    first += copies * HD

            def load_shift(b, m):
                sp.wait_ge(s_mt_ev, KC * b.n + m + 1)
                sp.dma_start(qst[b.odd][STACK:ROWS, m * HM:(m + 1) * HM, :], mts[m][:, :]).then_inc(d_shift[b.odd][m], 16)

            def load_expert(s, first, second, third):
                wait_count(sp, s_w_lo, s.n - 1)
                wait_count(sp, s_w2_lo, s.n - 1)
                for i, w in enumerate((first, second, third)):
                    sp.dma_start(w_raw[s.odd][:, i, :, :], w.rearrange("(c p) n -> p c n", p=P)).then_inc(d_w[s.odd], 16)

            sp.dma_start(x_all[:, :, :], x.rearrange("b q d -> q b d")).then_inc(d_x, 16)
            sp.wait_ge(s_const, 2)
            load_ctx(at(0))
            sp.dma_start(wkv_sb[:, 0, :, :], wk.rearrange("(c p) n -> p c n", p=P)).then_inc(d_wkv[0], 16)
            sp.dma_start(wkv_sb[:, 1, :, :], wv.rearrange("(c p) n -> p c n", p=P)).then_inc(d_wkv[1], 16)
            sp.dma_start(wq_sb[:, :, :], wq.rearrange("(c p) n -> p c n", p=P)).then_inc(d_wq, 16)
            sp.dma_start(bq_col[:, :], bq.rearrange("(c p) -> p c", p=P), allow_slow_non_contiguous=True).then_inc(d_bias, 16)
            sp.dma_start(bk_col[:, :], bk.rearrange("(c p) -> p c", p=P), allow_slow_non_contiguous=True).then_inc(d_bias, 16)
            load_ctx(at(1))
            sp.dma_start(wo_sb[:, :, :], wo.rearrange("(c p) n -> p c n", p=P)).then_inc(d_late, 16)
            sp.dma_start(bv_col[:, :], bv.rearrange("(c p) -> p c", p=P), allow_slow_non_contiguous=True).then_inc(d_late, 16)
            sp.dma_start(bo_rows[:, :], bo.partition_broadcast(SQ)).then_inc(d_late, 16)
            sp.dma_start(rw_sb[:, :, :], router_w.rearrange("(c p) e -> p c e", p=P)).then_inc(d_late, 16)
            sp.dma_start(eb_row[:, :], expert_bias.partition_broadcast(SQ)).then_inc(d_late, 16)
            sp.wait_ge(s_kones, 6)
            store_k(at(0), 0)
            store_q(0, 0)
            store_k(at(0), 1)
            store_q(0, 1)
            stack_k(at(0), 0)
            stack_q_parts(0)
            stack_k(at(0), 1)
            load_ctx(at(2))
            store_k(at(1), 0)
            store_k(at(1), 1)
            stack_k(at(1), 0)
            stack_k(at(1), 1)
            for m in range(KC):
                store_q(1, m)

            def iteration(i, load=True, first=False):
                load_shift(i, 1)
                if first:
                    stack_q_parts(1)
                if load:
                    load_ctx(i.plus(3))
                else:
                    load_expert(at(0), sw1, sw3, sw2)
                store_k(i.plus(2), 0)
                stack_k(i.plus(2), 0)
                load_shift(i.plus(1), 0)
                store_k(i.plus(2), 1)
                stack_k(i.plus(2), 1)

            load_shift(at(0), 0)
            iteration(at(0), first=True)
            with sp.Fori(0, B // 2 - 2) as pair:
                iteration(Step(pair, 0).plus(1))
                iteration(Step(pair, 1).plus(1))
            iteration(at(B - 3), load=False)
            load_shift(at(B - 2), 1)
            load_expert(at(1), w1[0], w3[0], w2[0])
            load_shift(at(B - 1), 0)
            load_shift(at(B - 1), 1)

            def load_gates(s):
                if not (isinstance(s.pair, int) and s.n < 3):
                    before = s.plus(-2)
                    sp.wait_ge(d_gate[s.odd], 16 * (before.pair + before.odd))
                sp.dma_start(gates[:, bass.ds(s.n - 1, 1), :].rearrange("p a t -> p (a t)"),
                             row_of(gate_dram, s.n - 1).partition_broadcast(P)).then_inc(d_gate[s.odd], 16)

            load_expert(at(2), w1[1], w3[1], w2[1])
            halves = [slice(half * HALF, (half + 1) * HALF) for half in range(2)]
            for half in range(2):
                sp.wait_ge(s_gt, half + 1)
                sp.dma_start(gate_dram[:, halves[half]], gateT[:, halves[half]]).then_inc(d_gt[half], 16)
            for half in range(2):
                sp.wait_ge(d_gt[half], 16)
                sp.dma_start(gates[:, 0, halves[half]], gate_dram[0, halves[half]].partition_broadcast(P)
                             ).then_inc((d_gate[at(1).odd], d_gate_rest)[half], 16)
            load_gates(at(2))
            with sp.Fori(0, E // 2 - 1) as pair:
                for odd in range(2):
                    s = Step(pair, odd).plus(3)
                    e = s.n - 1
                    load_expert(s, row(w1, e), row(w3, e), row(w2, e))
                    load_gates(s)
            for b in range(B):
                sp.wait_ge(s_acc, b + 1)
                sp.dma_start(out[b], x_all[:, b, :]).then_inc(d_out, 16)
            sp.wait_ge(d_out, 16 * B)

        @block.gpsimd
        def _(gp):
            gp.memset(ident[:, :], 0.0).then_inc(s_ones, 1)
            gp.memset(identb[:, :], 0.0).then_inc(s_ones, 1)
            gp.wait_ge(s_ones, 2)
            for t in (ident, identb):
                gp.affine_select(out=t[:, :], in_=t[:, :], compare_op=ALU.not_equal, fill=1.0, base=0,
                                 pattern=[[-1, P]], channel_multiplier=1).then_inc(s_ident, 1)
            gp.memset(half_neg[:, :], -0.5).then_inc(s_gp, 1)
            pair_of_ones = float(np.array([0x3F803F80], np.uint32).view(np.float32)[0])
            for i in range(2):
                gp.memset(kst[i][:, :, SK:SKP], 0.0).then_inc(s_kones, 1)
            gp.wait_ge(s_kones, 2)
            for i in range(2):
                gp.memset(kst[i][ONES:ROWS, :, SK - 1:SK], 1.0).then_inc(s_kones, 1)
                gp.memset(kst[i][ONES:ROWS, :, 0:SK - 1].bitcast(F32), pair_of_ones).then_inc(s_kones, 1)
            gp.wait_ge(s_kones, 6)
            def rstd_of(round_, batches):
                cols = slice(batches[0], batches[-1] + 1)
                gp.wait_ge(s_var, round_)
                gp.tensor_tensor(rstd[:, cols], var_eps[:, cols], half_neg[0:SQ, cols], ALU.pow).then_inc(s_rstd, 1)

            gp.wait_ge(s_gp, 1)
            for half in range(2):
                rstd_of(half + 1, half_batches(half))
            gp.wait_ge(s_const, 4)
            for i in range(2):
                v = vaug[i][:, TC - 1, :, :].rearrange("p h d -> p (h d)")
                gp.affine_select(out=v, in_=v, compare_op=ALU.is_ge, fill=0.0, base=LAST - 1,
                                 pattern=[[0, 2 * D]], channel_multiplier=-1).then_inc(s_gp, 1)
            gp.iota(experts_i[:, :, :], pattern=[[0, B], [1, E]], base=0, channel_multiplier=0).then_inc(s_iota, 1)
            def split_k(b):
                for m in range(KC):
                    n = 2 * (KC * b.n + m) + 3
                    gp.wait_ge(s_k_ev, KC * b.n + m + 1)
                    gp.tensor_tensor(kr[:, m, :], kf[:, m, :], kp[:, m, 0, :], ALU.subtract).then_inc(s_gp, 1)
                    gp.wait_ge(s_gp, n + 1)
                    wait_count(gp, d_k[m], 16 * b.n)
                    gp.sem_inc(s_apart, 1)
                    gp.tensor_copy(kp[:, m, 1, :], kr[:, m, :]).then_inc(s_gp, 1)
                    gp.wait_ge(s_gp, n + 2)
                    gp.tensor_tensor(kp[:, m, 2, :], kr[:, m, :], kp[:, m, 1, :], ALU.subtract).then_inc(s_kp, 1)

            split_k(at(0))
            split_k(at(1))
            with gp.Fori(0, B // 2 - 1) as pair:
                split_k(Step(pair, 0).plus(2))
                split_k(Step(pair, 1).plus(2))

            def cut_weights(s, n):
                gp.wait_ge(s_w_hi, s.n + 1)
                wait_count(gp, s_dn, 2 * (s.n - 1))
                gp.tensor_tensor(w_part[s.odd][1][:, 0:n, :, :], w_raw[s.odd][:, 0:n, :, :],
                                 w_part[s.odd][0][:, 0:n, :, :].bitcast(F32), ALU.subtract).then_inc(s_w_lo, 1)

            def cut_hidden(s, halves=range(2), weights=NW - 1):
                for half in halves:
                    if half == 1:
                        cut_weights(s.plus(1), weights)
                    u = 2 * s.n + half
                    gp.wait_ge(s_h_hi, u + 1)
                    wait_count(gp, s_dn, u - 1)
                    gp.tensor_tensor(h_part[half][1][:, :, :], hm[:, :, :],
                                     h_part[half][0][:, :, :].bitcast(F32), ALU.subtract).then_inc(s_h_lo, 1)

            cut_weights(at(0), NW)
            for n, batches in enumerate(LN2):
                rstd_of(n + 3, batches)
            cut_hidden(at(0), weights=NW)
            with gp.Fori(0, E // 2 - 1) as pair:
                for odd in range(2):
                    cut_hidden(Step(pair, odd).plus(1))
            cut_hidden(at(E - 1))
            cut_hidden(at(E), [0])

        @block.scalar
        def _(act):
            act.sem_inc(s_exp, EXP0)
            q_bank = [bank[4:6], bank[0:2]]

            def ctx_hi(b):
                wait_count(act, s_v_mm, 2 * (b.n - 1))
                for c in range(KC):
                    act.wait_ge(s_ct_mm, KC * b.n + c + 1)
                    act.activation(ct_part[b.odd][0][:, c, :], m_bank[c][:, 0:SKP], ACT.Copy).then_inc(s_ct_hi, 1)

            def xn_transposed(half):
                cols = slice(half * HALF, (half + 1) * HALF)
                for c in range(KC):
                    act.wait_ge(s_xt_mm, KC * half + c + 1)
                    act.activation(xnT[:, c, cols], bank[2 * half + c][:, 0:HALF], ACT.Copy).then_inc(s_xt, 1)

            def query(half):
                cols = slice(half * HALF, (half + 1) * HALF)
                for m in range(KC):
                    act.wait_ge(s_q_mm, KC * half + m + 1)
                    act.activation(qf[:, m, cols], q_bank[half][m][:, 0:HALF], ACT.Identity, bias=bq_col[:, m:m + 1])
                    act.activation(qp[:, 0, m, cols], q_bank[half][m][:, 0:HALF], ACT.Identity,
                                   bias=bq_col[:, m:m + 1]).then_inc(s_qf, 1)

            def evacuate_k(b, m):
                wait_count(act, s_kp, KC * (b.n - 1) + m + 1)
                wait_count(act, d_k[m], 16 * b.n)
                act.wait_ge(s_k_mm, KC * b.n + m + 1)
                act.activation(kf[:, m, :], g_bank[m][:, 0:SK], ACT.Identity, bias=bk_col[:, m:m + 1])
                act.activation(kp[:, m, 0, :], g_bank[m][:, 0:SK], ACT.Identity,
                               bias=bk_col[:, m:m + 1]).then_inc(s_k_ev, 1)

            def evacuate_v(b):
                wait_count(act, s_pv, G * (b.n - 1) + PV0)
                act.wait_ge(s_v_mm, 2 * b.n + 1)
                act.activation(vaug[b.odd][:, 0:TC - 1, :, HD:2 * HD],
                               g_bank[0][:, 0:(TC - 1) * D].rearrange("p (c h d) -> p c h d", h=H, d=HD),
                               ACT.Copy).then_inc(s_v_ev, 1)
                act.wait_ge(s_v_mm, 2 * b.n + 2)
                act.activation(vaug[b.odd][0:LAST, TC - 1, :, HD:2 * HD],
                               g_bank[1][0:LAST, 0:D].rearrange("p (h d) -> p h d", d=HD),
                               ACT.Copy).then_inc(s_v_ev, 1)

            def stack_q(b, m):
                if not (isinstance(b.pair, int) and b.n < 2):
                    act.wait_ge(s_s_mm, TC * (G * (b.n - 2) + G // KC * (m + 1)))
                heads = slice(m * HM, (m + 1) * HM)
                act.activation(qst[b.odd][0:STACK, heads, :],
                               qst_all[:, heads, bass.ds(b.n * SQ, SQ)], ACT.Copy).then_inc(s_qst, 1)

            def evacuate_shift(b, m):
                act.wait_ge(s_mt_mm, KC * b.n + m + 1)
                if not (isinstance(b.pair, int) and b.n == 0):
                    before = b.plus(-1)
                    act.wait_ge(d_shift[before.odd][m], 16 * (before.pair + 1))
                act.activation(mts[m][:, :], mt_bank[m], ACT.Copy).then_inc(s_mt_ev, 1)

            def exponentials(b, g, evacuate_next=False):
                act.wait_ge(s_pv, G * b.n + g - 1 + PV0)
                for n, c in enumerate(chunk_order(g)):
                    act.wait_ge(s_s_mm, TC * (G * b.n + g) + n + 1)
                    act.activation(probs[g % 2][:, c, :], s_bank[c][:, 0:GQ], ACT.Exp, scale=SCALE).then_inc(s_exp, 1)
                    if n == 1 and evacuate_next:
                        evacuate_shift(b.plus(1), 0)

            def evacuate_sums(b):
                act.wait_ge(s_pv, G * (b.n + 1) + PV0)
                act.activation(sums[:, :], o_bank[:, 0:G * SQ], ACT.Copy).then_inc(s_sums, 1)

            def evacuate_heads(b):
                act.wait_ge(s_ht_mm, b.n + 1)
                act.activation(headsT[:, :, :], g_bank[0][:, 0:KC * SQ].rearrange("p (c q) -> p c q", c=KC),
                               ACT.Copy).then_inc(s_ht, 1)

            def weights_hi(s):
                act.wait_ge(d_w[s.odd], 16 * NW * (s.pair + 1))
                wait_count(act, s_dn, 2 * (s.n - 1))
                act.activation(w_part[s.odd][0][:, :, :, :], w_raw[s.odd][:, :, :, :], ACT.Copy).then_inc(s_w_hi, 1)

            def xn2_hi(half):
                for c in range(KC):
                    act.wait_ge(s_x2_mm, KC * half + c + 1)
                    act.activation(xT_part[0][:, c, half * HALF:(half + 1) * HALF], m_bank[c][:, 0:HALF],
                                   ACT.Copy).then_inc(s_x2_hi, 1)

            ctx_hi(at(0))
            for i in range(2):
                act.wait_ge(d_wkv[i], 16)
                act.activation(wkv_part[0][:, i, :, :], wkv_sb[:, i, :, :], ACT.Copy).then_inc(s_wkv_hi, 1)
            act.wait_ge(d_bias, 32)
            evacuate_k(at(0), 0)
            xn_transposed(0)
            evacuate_k(at(0), 1)
            query(0)
            act.wait_ge(s_gp, 3)
            evacuate_v(at(0))
            ctx_hi(at(1))
            for m in range(KC):
                evacuate_k(at(1), m)
            xn_transposed(1)
            query(1)
            act.wait_ge(d_qst[0], 16 * STACK // HD)
            stack_q(at(0), 0)
            stack_q(at(0), 1)
            stack_q(at(1), 0)

            def iteration(i, project=True, maxima=True, before=True):
                if project:
                    ctx_hi(i.plus(2))
                evacuate_shift(i, 1)
                if before:
                    evacuate_sums(i.plus(-1))
                if project:
                    evacuate_v(i.plus(1))
                if not maxima:
                    evacuate_v(i)
                for g in range(G):
                    exponentials(i, g, evacuate_next=maxima and g == G - 1)
                    if g == 0 and project:
                        for m in range(KC):
                            evacuate_k(i.plus(2), m)
                    if g == 0 and maxima:
                        stack_q(i.plus(1), 1)
                    if g == 1 and before:
                        evacuate_heads(i.plus(-1))
                    if g == 2 and project:
                        stack_q(i.plus(2), 0)
                    if g == 2 and not maxima:
                        xn2_hi(0)

            evacuate_shift(at(0), 0)
            iteration(at(0), before=False)
            act.wait_ge(d_qst[1], 16 * STACK // HD)
            with act.Fori(0, B // 2 - 2) as pair:
                iteration(Step(pair, 0).plus(1))
                iteration(Step(pair, 1).plus(1))
            iteration(at(B - 3))
            weights_hi(at(0))
            act.wait_ge(d_late, 16 * LATE)
            act.activation(rw_part[0][:, :, :], rw_sb[:, :, :], ACT.Copy).then_inc(s_rw_hi, 1)
            iteration(at(B - 2), project=False)
            iteration(at(B - 1), project=False, maxima=False)

            def expert_half(s, half, cut_next=True, between=None, by_chunk=False):
                if half == 1 and cut_next:
                    weights_hi(s.plus(1))
                u = 2 * s.n + half
                wait_count(act, s_hm, FC * u)
                for m in range(FC):
                    act.wait_ge(s_up, FC * u + m + 1)
                    act.activation(sil[:, m, :], up_bank[m][0][:, 0:HALF], ACT.Silu).then_inc(s_sil, 1)
                if between:
                    between()
                wait_count(act, s_dn, u - 1)
                chunks = [slice(m, m + 1) for m in range(FC)] if by_chunk else [slice(0, FC)]
                for chunk in chunks:
                    act.wait_ge(s_hm, FC * u + chunk.stop)
                    act.activation(h_part[half][0][:, chunk, :], hm[:, chunk, :], ACT.Copy).then_inc(s_h_hi, 1)

            def expert(s):
                for half in range(2):
                    expert_half(s, half)

            evacuate_sums(at(B - 1))
            evacuate_heads(at(B - 1))
            def gates_transposed():
                for half in range(2):
                    act.wait_ge(s_gt_mm, half + 1)
                    act.activation(gateT[:, half * HALF:(half + 1) * HALF], g_bank[half][0:E, 0:HALF],
                                   ACT.Copy).then_inc(s_gt, 1)

            def logits_transposed(half):
                act.wait_ge(s_lt_mm, half + 1)
                act.activation(logitsT[:, half * HALF:(half + 1) * HALF], logits_bank[half][0:E, 0:HALF], ACT.Copy).then_inc(s_lt, 1)

            def second_half_ready():
                xn2_hi(1)
                logits_transposed(0)
                logits_transposed(1)

            expert_half(at(0), 0, between=second_half_ready)
            act.wait_ge(s_lg, 1)
            act.activation(ex[:, :, :], logits[:, :, :], ACT.Exp).then_inc(s_ex, 1)
            expert_half(at(0), 1, between=gates_transposed)
            with act.Fori(0, E // 2 - 1) as pair:
                for odd in range(2):
                    expert(Step(pair, odd).plus(1))
            expert(at(E - 1))
            expert_half(at(E), 0)
            expert_half(at(E), 1, cut_next=False, by_chunk=True)
            for half in range(2):
                for m in range(KC):
                    act.wait_ge(s_dn, 2 * E + KC * half + m + 1)
                    act.activation(y_sb[half][:, m, :], y_bank[half][m][:, 0:HALF], ACT.Copy).then_inc(s_y, 1)

        @block.tensor
        def _(pe):
            def ctx_transposes(b):
                pe.wait_ge(d_cx[b.odd], 32 * (b.pair + 1))
                wait_count(pe, s_m_rd, H * (b.n - 1))
                for c in range(KC):
                    for t in range(TC):
                        mm = pe.transpose(m_bank[c][:, t * P:(t + 1) * P], cx[b.odd][:, t, c * P:(c + 1) * P], ident[:, :])
                    mm.then_inc(s_ct_mm, 1)

            def project_k(b, m):
                if m == 0:
                    pe.wait_ge(s_ct_lo, KC * (b.n + 1))
                wait_count(pe, s_v_ev, 2 * b.n - 1 + m)
                n = 0
                for c in range(KC):
                    for wi, ci in PASSES:
                        mm = pe.matmul(g_bank[m][:, 0:SKE], wkv_part[wi][:, 0, c, m * P:(m + 1) * P],
                                       ct_part[b.odd][ci][:, c, 0:SKE], start=(n == 0), stop=(n == KC * len(PASSES) - 1))
                        n += 1
                mm.then_inc(s_k_mm, 1)

            def project_v(b, chunks=range(TC), ahead=2):
                for t in chunks:
                    if t == 0:
                        pe.wait_ge(s_k_ev, KC * (b.n + 1))
                        if not (isinstance(b.pair, int) and b.n < 2):
                            pe.wait_ge(s_o_ev, b.n - ahead + O0)
                    if t == TC - 1 and not (isinstance(b.pair, int) and b.n < 2):
                        pe.wait_ge(s_m_rd, H * (b.n + 1 - ahead) + MID.stop)
                    dst = g_bank[0][:, t * D:(t + 1) * D] if t < TC - 1 else g_bank[1][:, 0:D]
                    n = 0
                    for c in range(KC):
                        for ci, wi in PASSES:
                            mm = pe.matmul(dst, ct_part[b.odd][ci][:, c, t * P:(t + 1) * P], wkv_part[wi][:, 1, c, :],
                                           start=(n == 0), stop=(n == KC * len(PASSES) - 1))
                            n += 1
                    if t >= TC - 2:
                        mm.then_inc(s_v_mm, 1)

            def max_scores(b, h, banks=max_banks):
                if banks[h] in banks[:h]:
                    last = max(k for k in range(h) if banks[k] == banks[h])
                    pe.wait_ge(s_m_rd, H * b.n + last + 1)
                pe.matmul(bank[banks[h]][0:SQ, 0:SK], qst[b.odd][0:STACK, h, :], kst[b.odd][0:STACK, h, 0:SK],
                          start=True, stop=True).then_inc(s_m_mm, 1)

            def shift_transpose(b, m):
                pe.wait_ge(s_mp, KC * b.n + m + 1)
                wait_count(pe, s_mt_ev, KC * (b.n - 1) + m + 1)
                pe.sem_inc(s_apart, 1)
                pe.transpose(mt_bank[m], mp[m][:, :, :].rearrange("q s h -> q (s h)"),
                             identb[0:SQ, 0:SQ]).then_inc(s_mt_mm, 1)

            def scores(b, g, n):
                c = chunk_order(g)[n]
                pe.wait_ge(s_exp, TC * (G * b.n + g - 1) + chunk_order(g - 1).index(c) + 1 + EXP0)
                for j in range(HG):
                    h = HG * g + j
                    mm = pe.matmul(s_bank[c][:, j * SQ:(j + 1) * SQ], kst[b.odd][0:ROWS, h, c * P:(c + 1) * P],
                                   qst[b.odd][0:ROWS, h, :], start=True, stop=True)
                mm.then_inc(s_s_mm, 1)

            def context(b, g):
                for n, c in enumerate(chunk_order(g)):
                    pe.wait_ge(s_exp, TC * (G * b.n + g) + n + 1 + EXP0)
                    for j in range(HG):
                        mm = pe.matmul(o_bank[32 * j:32 * j + 32, g * SQ:(g + 1) * SQ],
                                       vaug[b.odd][:, c, HG * g + j, :], probs[g % 2][:, c, j * SQ:(j + 1) * SQ],
                                       start=(n == 0), stop=(n == TC - 1))
                mm.then_inc(s_pv, 1)

            def transpose_sums(b):
                pe.wait_ge(s_sums, b.n + 1)
                for g in range(G):
                    mm = pe.transpose(o_bank[0:SQ, g * P:(g + 1) * P], sums[:, g * SQ:(g + 1) * SQ], ident[:, :])
                mm.then_inc(s_sums_mm, 1)

            def transpose_heads(b, bank_free):
                pe.wait_ge(s_norm, b.n + 1)
                pe.wait_ge(*bank_free)
                rows = heads_q[:, :, :].rearrange("q h d -> q (h d)")
                for c in range(KC):
                    mm = pe.transpose(g_bank[0][:, c * SQ:(c + 1) * SQ], rows[:, c * P:(c + 1) * P], ident[0:SQ, 0:SQ])
                mm.then_inc(s_ht_mm, 1)

            def attn_out(b):
                pe.wait_ge(s_ht, b.n + 1)
                for c in range(KC):
                    mm = pe.matmul(g_bank[0][0:SQ, 0:D], headsT[:, c, :], wo_sb[:, c, :], start=(c == 0), stop=(c == KC - 1))
                mm.then_inc(s_o_mm, 1)

            pe.sem_inc(s_pv, PV0)
            pe.wait_ge(s_ident, 2)
            q_bank = [bank[4:6], bank[0:2]]

            def xn_transposes(half):
                pe.wait_ge(s_xn, HB * (half + 1))
                for c in range(KC):
                    for j, b in enumerate(half_batches(half)):
                        mm = pe.transpose(bank[2 * half + c][:, j * SQ:(j + 1) * SQ], xn[:, b, c * P:(c + 1) * P],
                                          ident[0:SQ, 0:SQ])
                    mm.then_inc(s_xt_mm, 1)

            def query(half):
                pe.wait_ge(d_wq, 16)
                pe.wait_ge(s_xt, KC * (half + 1))
                for m in range(KC):
                    for c in range(KC):
                        mm = pe.matmul(q_bank[half][m][:, 0:HALF], wq_sb[:, c, m * P:(m + 1) * P],
                                       xnT[:, c, half * HALF:(half + 1) * HALF], start=(c == 0), stop=(c == KC - 1))
                    mm.then_inc(s_q_mm, 1)

            ctx_transposes(at(0))
            pe.wait_ge(s_wkv_lo, 1)
            project_k(at(0), 0)
            xn_transposes(0)
            project_k(at(0), 1)
            query(0)
            pe.wait_ge(s_wkv_lo, 2)
            project_v(at(0))
            pe.wait_ge(s_qf, KC)
            ctx_transposes(at(1))
            pe.wait_ge(s_bv, 1)
            for c in range(KC):
                mm = pe.matmul(o_bank[0:SQ, 0:D], bv_wide[:, c, :], wo_sb[:, c, :], start=(c == 0), stop=(c == KC - 1))
            mm.then_inc(s_bias_mm, 1)
            for m in range(KC):
                project_k(at(1), m)
            pe.wait_ge(s_bias, 1)
            xn_transposes(1)
            query(1)
            project_v(at(1), [0])
            pe.wait_ge(s_qf, 2 * KC)
            for m in range(KC):
                pe.wait_ge(s_qst, m + 1)
                pe.wait_ge(d_kst[0][m], 16 * len(RUNS))
                for h in range(m * HM, (m + 1) * HM):
                    max_scores(at(0), h, first_max_banks)
                    if h == HM:
                        project_v(at(1), [1])
            shift_transpose(at(0), 0)
            project_v(at(1), [2])

            def xn2_transposes(half):
                pe.wait_ge(s_xn2, HB * (half + 1))
                if half == 0:
                    pe.wait_ge(s_m_rd, H * B)
                    pe.wait_ge(s_mt_ev, KC * B)
                for c in range(KC):
                    for j, b in enumerate(half_batches(half)):
                        mm = pe.transpose(m_bank[c][:, j * SQ:(j + 1) * SQ], xn[:, b, c * P:(c + 1) * P], ident[0:SQ, 0:SQ])
                    mm.then_inc(s_x2_mm, 1)

            def iteration(i, project=True, maxima=True, before=True, ahead=2):
                if project:
                    ctx_transposes(i.plus(2))
                if before:
                    pe.wait_ge(s_mt_ev, KC * i.n + 1)
                    context(i.plus(-1), G - 1)
                shift_transpose(i, 1)
                for g in range(G):
                    if g % (G // KC) == 0:
                        pe.wait_ge(d_shift[i.odd][g // (G // KC)], 16 * (i.pair + 1))

                    def maximum(j):
                        h = HG * g + j
                        if maxima and h % HM == 0:
                            m = h // HM
                            pe.wait_ge(d_kst[i.plus(1).odd][m], 16 * len(RUNS) * (i.plus(1).pair + 1))
                            pe.wait_ge(s_qst, KC * (i.n + 1) + m + 1)
                        if maxima and max_banks[h] not in max_banks[:h] and max_banks[h] == 7:
                            pe.wait_ge(s_k_ev, KC * (i.n + 3) if project else KC * B)
                        if maxima:
                            max_scores(i.plus(1), h)

                    if g == 0:
                        for n in range(TC):
                            if n == TC - 1:
                                pe.wait_ge(s_mt_ev, KC * (i.n + 1))
                            scores(i, g, n)
                        if project:
                            pe.wait_ge(s_ct_lo, KC * (i.n + 3))
                        maximum(0)
                        maximum(1)
                        if before:
                            transpose_sums(i.plus(-1))
                        if project:
                            project_k(i.plus(2), 0)
                        maximum(2)
                        if project:
                            project_k(i.plus(2), 1)
                        maximum(3)
                        maximum(4)
                        continue
                    scores(i, g, 0)
                    if g > 1:
                        maximum(0)
                    if g == 1:
                        if before:
                            pe.wait_ge(s_norm, i.n)
                        pe.wait_ge(s_v_ev, 2 * (i.n + 1))
                    context(i, g - 1)
                    if g == 1 and before:
                        transpose_heads(i.plus(-1), (s_k_ev, KC * (i.n + 2) + 1) if project else (s_o_ev, i.n - 1 + O0))
                    scores(i, g, 1)
                    maximum(1)
                    if g == G - 1 and maxima:
                        shift_transpose(i.plus(1), 0)
                    if g == 2 and before:
                        attn_out(i.plus(-1))
                    if g == G - 1 and ahead:
                        project_v(i.plus(ahead), [0], ahead)
                    scores(i, g, 2)
                    maximum(2)
                    if g == G - 1 and ahead:
                        project_v(i.plus(ahead), [1], ahead)
                    if g == 2 and not maxima:
                        xn2_transposes(0)
                    maximum(3)
                    if g == G - 1 and ahead:
                        project_v(i.plus(ahead), range(2, TC), ahead)

            iteration(at(0), before=False)
            with pe.Fori(0, B // 2 - 2) as pair:
                iteration(Step(pair, 0).plus(1))
                iteration(Step(pair, 1).plus(1))
            iteration(at(B - 3), ahead=0)
            iteration(at(B - 2), project=False, ahead=1)
            iteration(at(B - 1), project=False, maxima=False, ahead=0)
            context(at(B - 1), G - 1)

            def logits_of(half):
                n = 0
                for c in range(KC):
                    for wi, xi in PASSES:
                        mm = pe.matmul(logits_bank[half][0:E, 0:HALF], rw_part[wi][:, c, :],
                                       xT_part[xi][:, c, half * HALF:(half + 1) * HALF],
                                       start=(n == 0), stop=(n == KC * len(PASSES) - 1))
                        n += 1
                mm.then_inc(s_lt_mm, 1)

            def logits_transposes():
                pe.wait_ge(s_lt, 2)
                for b in range(B):
                    mm = pe.transpose(g_bank[1][0:SQ, b * E:(b + 1) * E], logitsT[:, b * SQ:(b + 1) * SQ], ident[0:E, 0:E])
                mm.then_inc(s_lg_mm, 1)

            def up_product(s, half, m, w):
                u = 2 * s.n + half
                if w == 0:
                    wait_count(pe, s_hm, FC * (u - 1) + m + 1)
                n = 0
                for c in range(KC):
                    for wi, xi in PASSES:
                        mm = pe.matmul(up_bank[m][w][:, 0:HALF], w_part[s.odd][wi][:, w, c, m * P:(m + 1) * P],
                                       xT_part[xi][:, c, half * HALF:(half + 1) * HALF],
                                       start=(n == 0), stop=(n == KC * len(PASSES) - 1))
                        n += 1
                if w == 1:
                    mm.then_inc(s_up, 1)

            def up(s, half):
                if half == 0:
                    pe.wait_ge(s_w_lo, s.n + 1)
                for m in range(FC):
                    for w in range(2):
                        up_product(s, half, m, w)

            def down(s, half, first=False, last=False):
                u = 2 * s.n + half
                pe.wait_ge(s_h_lo, u + 1)
                pe.wait_ge(s_w2_lo, s.n + 1)
                for m in range(KC):
                    n = 0
                    for c in range(FC):
                        if last and half and m == 0 and c:
                            pe.wait_ge(s_h_lo, u + 1 + c)
                        for wi, hi in PASSES:
                            mm = pe.matmul(y_bank[half][m][:, 0:HALF], w_part[s.odd][wi][:, 2, c, m * P:(m + 1) * P],
                                           h_part[half][hi][:, c, :], start=(first and n == 0),
                                           stop=(last and n == FC * len(PASSES) - 1))
                            n += 1
                    if last or m == KC - 1:
                        mm.then_inc(s_dn, 1)
                    if last and half and m == 0:
                        y_transposes(0)

            def gate_transposes():
                pe.wait_ge(s_gate, 1)
                pe.wait_ge(s_o_ev, B + O0)
                for half in range(2):
                    for j, b in enumerate(half_batches(half)):
                        mm = pe.transpose(g_bank[half][0:E, j * SQ:(j + 1) * SQ], gate[:, b, :], ident[0:SQ, 0:SQ])
                    mm.then_inc(s_gt_mm, 1)

            def y_transposes(half):
                pe.wait_ge(s_y, KC * (half + 1))
                pe.wait_ge(s_hm, FC * 2 * (E + 1))
                for j, b in enumerate(half_batches(half)):
                    wait_count(pe, s_acc, b - HB + 1)
                    for m in range(KC):
                        mm = pe.transpose(bank[j][0:SQ, m * P:(m + 1) * P], y_sb[half][:, m, j * SQ:(j + 1) * SQ],
                                          ident[:, :])
                    mm.then_inc(s_yt_mm, 1)

            pe.wait_ge(s_x2_lo, KC)
            pe.wait_ge(s_w_lo, 1)
            pe.wait_ge(s_exp, TC * G * B + EXP0)
            up_product(at(0), 0, 0, 0)
            transpose_sums(at(B - 1))
            up_product(at(0), 0, 0, 1)
            transpose_heads(at(B - 1), (s_o_ev, B - 1 + O0))
            up_product(at(0), 0, 1, 0)
            attn_out(at(B - 1))
            up_product(at(0), 0, 1, 1)
            pe.wait_ge(s_rw_lo, 1)
            xn2_transposes(1)
            logits_of(0)
            pe.wait_ge(s_x2_lo, 2 * KC)
            logits_of(1)
            for w in range(2):
                up_product(at(0), 1, 0, w)
            logits_transposes()
            for w in range(2):
                up_product(at(0), 1, 1, w)
            down(at(0), 0, first=True)
            gate_transposes()
            up(at(1), 0)
            pe.wait_ge(s_gt, 2)
            down(at(0), 1, first=True)
            up(at(1), 1)
            down(at(1), 0)
            with pe.Fori(0, E // 2 - 1) as pair:
                for odd in range(2):
                    s = Step(pair, odd).plus(2)
                    up(s, 0)
                    down(s.plus(-1), 1)
                    up(s, 1)
                    down(s, 0)
            up(at(E), 0)
            down(at(E - 1), 1)
            up(at(E), 1)
            down(at(E), 0, last=True)
            down(at(E), 1, last=True)
            y_transposes(1)

        @block.vector
        def _(ve):
            chain = [0]

            def link(ins):
                chain[0] += 1
                ins.then_inc(s_vec, 1)
                ve.wait_ge(s_vec, chain[0])

            ve.sem_inc(s_o_ev, O0)
            ve.sem_inc(s_w2_lo, W0)
            for i in range(2):
                ve.memset(cx[i][:, TC - 1, :], 0.0).then_inc(s_const, 1)
            for i in range(2):
                ve.memset(vaug[i][:, :, :, :], 1.0).then_inc(s_const, 1)

            def row_stats(b):
                r = x_all[:, bass.ds(b, 1), :].rearrange("q a d -> q (a d)")
                return ve.bn_stats(stats[:, bass.ds(b, 1), :].rearrange("q a s -> q (a s)"), r)

            def var_and_eps(batches):
                first, last = batches[0], batches[-1]
                for b in batches:
                    ins = row_stats(b)
                link(ins)
                for b in batches:
                    ins = ve.bn_aggr(mv[:, b, :], stats[:, b, :])
                link(ins)
                ve.tensor_scalar(var_eps[:, first:last + 1], mv[:, first:last + 1, 1], EPS, None, ALU.add).then_inc(s_var, 1)

            def normalise_x(ready, round_, batches):
                ve.wait_ge(s_rstd, round_)
                for b in batches:
                    ve.tensor_scalar(xn[:, b, :], x_all[:, b, :], mv[:, b, 0:1], rstd[:, b:b + 1],
                                     ALU.subtract, ALU.mult).then_inc(ready, 1)

            def cut_query(half):
                cols = slice(half * HALF, (half + 1) * HALF)
                for m in range(KC):
                    ve.wait_ge(s_qf, KC * half + m + 1)
                    link(ve.tensor_tensor(qr[:, m, cols], qf[:, m, cols], qp[:, 0, m, cols], ALU.subtract))
                    link(ve.tensor_copy(qp[:, 1, m, cols], qr[:, m, cols]))
                    ve.tensor_tensor(qp[:, 2, m, cols], qr[:, m, cols], qp[:, 1, m, cols], ALU.subtract).then_inc(s_qp, 1)

            def ctx_lo(b):
                for c in range(KC):
                    ve.wait_ge(s_ct_hi, KC * b.n + c + 1)
                    ve.tensor_tensor(ct_part[b.odd][1][:, c, :], m_bank[c][:, 0:SKP],
                                     ct_part[b.odd][0][:, c, :].bitcast(F32), ALU.subtract).then_inc(s_ct_lo, 1)

            def reduce_max(b, h, banks=max_banks):
                ve.wait_ge(s_m_mm, H * b.n + h + 1)
                ve.tensor_reduce(negm[:, h:h + 1], bank[banks[h]][0:SQ, 0:SK], AX_X, ALU.max,
                                 negate=True).then_inc(s_m_rd, 1)

            def cut_shift(b, m, step):
                n = 3 * (KC * b.n + m)
                heads = slice(m * HM, (m + 1) * HM)
                if step == 0:
                    ve.wait_ge(s_m_rd, H * b.n + (m + 1) * HM)
                    wait_count(ve, s_mt_mm, KC * (b.n - 1) + m + 1)
                    ve.tensor_copy(mp[m][:, 0, :], negm[:, heads]).then_inc(s_step, 1)
                elif step == 1:
                    ve.wait_ge(s_step, n + 1)
                    ve.tensor_tensor(negm_r[:, heads], negm[:, heads], mp[m][:, 0, :], ALU.subtract).then_inc(s_step, 1)
                elif step == 2:
                    ve.wait_ge(s_step, n + 2)
                    ve.tensor_copy(mp[m][:, 1, :], negm_r[:, heads]).then_inc(s_step, 1)
                else:
                    ve.wait_ge(s_step, n + 3)
                    ve.tensor_tensor(mp[m][:, 2, :], negm_r[:, heads], mp[m][:, 1, :], ALU.subtract).then_inc(s_mp, 1)

            def maxima_and_shifts(b, before=False, banks=max_banks):
                for h in range(H):
                    reduce_max(b, h, banks)
                    if h == 1 and before:
                        normalise(b.plus(-2))
                    if HM <= h < HM + 4:
                        cut_shift(b, 0, h - HM)
                    if h == H - 5 and before:
                        add_attn_out(b.plus(-2))
                for step in range(4):
                    cut_shift(b, 1, step)

            def normalise(b):
                ve.wait_ge(s_sums_mm, b.n + 1)
                both = o_bank[0:SQ, 0:2 * D].rearrange("q (h w) -> q h w", h=H)
                ve.reciprocal(rden[:, :], both[:, :, 0]).then_inc(s_nrm, 1)
                ve.wait_ge(s_nrm, b.n + 1)
                ve.tensor_tensor(heads_q[:, :, :], both[:, :, HD:2 * HD],
                                 rden[:, :].unsqueeze(2).to_broadcast([SQ, H, HD]), ALU.mult).then_inc(s_norm, 1)

            def add_attn_out(b):
                ve.wait_ge(s_o_mm, b.n + 1)
                row = x_all[:, bass.ds(b.n, 1), :].rearrange("q a d -> q (a d)")
                ve.tensor_tensor(row, g_bank[0][0:SQ, 0:D], row, ALU.add).then_inc(s_o_ev, 1)

            def weights_lo(i):
                ve.wait_ge(s_wkv_hi, i + 1)
                ve.tensor_tensor(wkv_part[1][:, i, :, :], wkv_sb[:, i, :, :], wkv_part[0][:, i, :, :].bitcast(F32),
                                 ALU.subtract).then_inc(s_wkv_lo, 1)

            ve.wait_ge(d_x, 16)
            for half in range(2):
                var_and_eps(half_batches(half))
            ctx_lo(at(0))
            weights_lo(0)
            for half in range(2):
                normalise_x(s_xn, half + 1, half_batches(half))
            weights_lo(1)
            ve.wait_ge(d_late, 16 * LATE)
            ve.tensor_copy(bv_wide[:, :, :], bv_col[:, :].unsqueeze(2).to_broadcast([P, KC, SQ])).then_inc(s_bv, 1)
            cut_query(0)
            ctx_lo(at(1))
            ve.wait_ge(s_bias_mm, 1)
            ve.tensor_tensor(out_bias[:, :], o_bank[0:SQ, 0:D], bo_rows[:, :], ALU.add).then_inc(s_bias, 1)
            ve.wait_ge(s_bias, 1)
            link(ve.tensor_tensor(x_all[:, :, :], x_all[:, :, :],
                                  out_bias[:, :].unsqueeze(1).to_broadcast([SQ, B, D]), ALU.add))
            cut_query(1)
            maxima_and_shifts(at(0), banks=first_max_banks)

            def iteration(i, project=True, maxima=True, before=True):
                if project:
                    ctx_lo(i.plus(2))
                if maxima:
                    maxima_and_shifts(i.plus(1), before)
                elif before:
                    normalise(i.plus(-1))

            iteration(at(0), before=False)
            with ve.Fori(0, B // 2 - 2) as pair:
                iteration(Step(pair, 0).plus(1))
                iteration(Step(pair, 1).plus(1))
            iteration(at(B - 3))
            iteration(at(B - 2), project=False)
            iteration(at(B - 1), project=False, maxima=False)
            def xn2_lo(half):
                cols = slice(half * HALF, (half + 1) * HALF)
                for c in range(KC):
                    ve.wait_ge(s_x2_hi, KC * half + c + 1)
                    ve.tensor_tensor(xT_part[1][:, c, cols], m_bank[c][:, 0:HALF], xT_part[0][:, c, cols].bitcast(F32),
                                     ALU.subtract).then_inc(s_x2_lo, 1)

            def hidden(s, half):
                u = 2 * s.n + half
                wait_count(ve, s_h_lo, u)
                for m in range(FC):
                    ve.wait_ge(s_sil, FC * u + m + 1)
                    ve.tensor_tensor(hm[:, m, :], up_bank[m][1][:, 0:HALF], sil[:, m, :], ALU.mult).then_inc(s_hm, 1)

            ve.wait_ge(s_o_ev, HB + O0)
            var_and_eps(LN2[0])
            ve.wait_ge(d_late, 16 * LATE)
            ve.wait_ge(s_rw_hi, 1)
            ve.tensor_tensor(rw_part[1][:, :, :], rw_sb[:, :, :], rw_part[0][:, :, :].bitcast(F32),
                             ALU.subtract).then_inc(s_rw_lo, 1)
            ve.wait_ge(s_iota, 1)
            link(ve.tensor_copy(experts[:, :, :], experts_i[:, :, :]))
            normalise_x(s_xn2, 3, LN2[0])
            add_attn_out(at(B - 2))
            xn2_lo(0)
            ve.wait_ge(s_o_ev, B - 1 + O0)
            var_and_eps(LN2[1])
            normalise(at(B - 1))
            normalise_x(s_xn2, 4, LN2[1])
            add_attn_out(at(B - 1))
            ve.wait_ge(s_o_ev, B + O0)
            var_and_eps(LN2[2])
            normalise_x(s_xn2, 5, LN2[2])
            hidden(at(0), 0)
            xn2_lo(1)

            def wide(t):
                return t.unsqueeze(2).to_broadcast([SQ, B, E])

            ve.wait_ge(s_lg_mm, 1)
            lg = g_bank[1][0:SQ, 0:B * E].rearrange("q (b e) -> q b e", e=E)
            link(ve.tensor_reduce(rowmax[:, :], lg, AX_X, ALU.max))
            ve.tensor_tensor(logits[:, :, :], lg, wide(rowmax[:, :]), ALU.subtract).then_inc(s_lg, 1)
            ve.wait_ge(s_ex, 1)
            link(ve.tensor_reduce(esum[:, :], ex[:, :, :], AX_X, ALU.add))
            link(ve.reciprocal(erec[:, :], esum[:, :]))
            link(ve.tensor_tensor(score[:, :, :], ex[:, :, :], wide(erec[:, :]), ALU.mult))
            link(ve.tensor_tensor(biased[:, :, :], score[:, :, :], eb_row[:, :].unsqueeze(1).to_broadcast([SQ, B, E]), ALU.add))
            for b in range(B - 1):
                ve.max(top8[:, b, :], biased[:, b, :])
            link(ve.max(top8[:, B - 1, :], biased[:, B - 1, :]))
            for b in range(B - 1):
                ve.max_index(top8_i[:, b, :], top8[:, b, :], biased[:, b, :])
            link(ve.max_index(top8_i[:, B - 1, :], top8[:, B - 1, :], biased[:, B - 1, :]))
            link(ve.tensor_copy(top8_f[:, :, :], top8_i[:, :, :]))
            link(ve.tensor_tensor(is_first[:, :, :], experts[:, :, :],
                                  top8_f[:, :, 0:1].to_broadcast([SQ, B, E]), ALU.is_equal))
            link(ve.tensor_tensor(is_second[:, :, :], experts[:, :, :],
                                  top8_f[:, :, 1:2].to_broadcast([SQ, B, E]), ALU.is_equal))
            link(ve.tensor_tensor(chosen[:, :, :], is_first[:, :, :], is_second[:, :, :], ALU.add))
            ve.tensor_tensor(gate[:, :, :], chosen[:, :, :], score[:, :, :], ALU.mult).then_inc(s_gate, 1)
            hidden(at(0), 1)

            def gated_hidden(s, half):
                u = 2 * s.n + half
                wait_count(ve, s_h_lo, u)
                for m in range(FC):
                    ve.wait_ge(s_up, FC * u + m + 1)
                    ve.tensor_tensor(gated[:, m, :], up_bank[m][1][:, 0:HALF],
                                     gates[:, bass.ds(s.n - 1, 1), half * HALF:(half + 1) * HALF].rearrange(
                                         "p a t -> p (a t)"), ALU.mult).then_inc(s_gated, 1)
                    ve.wait_ge(s_gated, FC * (u - 2) + m + 1)
                    ve.wait_ge(s_sil, FC * u + m + 1)
                    ve.tensor_tensor(hm[:, m, :], gated[:, m, :], sil[:, m, :], ALU.mult).then_inc(s_hm, 1)

            def cut_third_weights(s):
                ve.wait_ge(s_w_hi, s.n + 1)
                ve.tensor_tensor(w_part[s.odd][1][:, NW - 1, :, :], w_raw[s.odd][:, NW - 1, :, :],
                                 w_part[s.odd][0][:, NW - 1, :, :].bitcast(F32), ALU.subtract).then_inc(s_w2_lo, 1)

            def expert(s, last=False):
                ve.wait_ge(d_gate[s.odd], 16 * (s.pair + s.odd))
                gated_hidden(s, 0)
                if not last:
                    cut_third_weights(s.plus(1))
                ve.wait_ge(d_gate_rest, 16)
                gated_hidden(s, 1)

            with ve.Fori(0, E // 2 - 1) as pair:
                for odd in range(2):
                    expert(Step(pair, odd).plus(1))
            expert(at(E - 1))
            expert(at(E), last=True)
            for m in range(FC):
                ve.wait_ge(s_h_hi, 2 * E + 2 + m)
                wait_count(ve, s_dn, 2 * E)
                ve.tensor_tensor(h_part[1][1][:, m, :], hm[:, m, :], h_part[1][0][:, m, :].bitcast(F32),
                                 ALU.subtract).then_inc(s_h_lo, 1)
            for b in range(B):
                ve.wait_ge(s_yt_mm, b + 1)
                ve.tensor_tensor(x_all[:, b, :], bank[b % HB][0:SQ, 0:D], x_all[:, b, :], ALU.add).then_inc(s_acc, 1)


_INS = ['x', 'ctx_1024', 'L0_xattn_Wq', 'L0_xattn_bq', 'L0_xattn_Wk', 'L0_xattn_bk', 'L0_xattn_Wv', 'L0_xattn_bv',
        'L0_xattn_Wo', 'L0_xattn_bo', 'L0_ffn_router_w', 'L0_ffn_expert_bias', 'L0_ffn_w1', 'L0_ffn_w2', 'L0_ffn_w3',
        'L0_ffn_sw1', 'L0_ffn_sw2', 'L0_ffn_sw3']


def kernel(**inputs):
    import numpy as _np
    import concourse.bacc as _bacc
    from concourse import mybir as _mybir
    from concourse.bass_utils import run_bass_kernel_spmd as _run

    nc = _bacc.Bacc("TRN2", target_bir_lowering=False, num_devices=1)
    arrays, args = {}, []
    for name in _INS:
        a = _np.ascontiguousarray(inputs[name])
        arrays[f"in_{name}_dram"] = a
        args.append(nc.dram_tensor(f"in_{name}_dram", a.shape, _mybir.dt.from_np(a.dtype), kind="ExternalInput").ap())
    shape = _np.shape(inputs['x'])
    args.append(nc.dram_tensor("out_0_dram", shape, _mybir.dt.float32, kind="ExternalOutput").ap())
    xattn_ffn(nc, *args)
    r = _run(nc, [arrays], core_ids=[0])
    return r.results[0]["out_0_dram"]
```
